# Optimizing a Trainium2 kernel written in Bass

```python
import numpy as np
import jax
import jax.numpy as jnp

def _softmax(x, axis=-1):
    return jax.nn.softmax(x, axis=axis)

def _gelu(x):
    return jax.nn.gelu(x, approximate=True)

def _silu(x):
    return jax.nn.silu(x)

def _sigmoid(x):
    return jax.nn.sigmoid(x)

def _layernorm(x, axis=-1, eps=1e-05):
    m = jnp.mean(x, axis=axis, keepdims=True)
    v = jnp.var(x, axis=axis, keepdims=True)
    return (x - m) / jnp.sqrt(v + eps)

def _scatter_add(tgt, idx, src, axis=0):
    return tgt.at[idx].add(src)

def _segment_sum(src, seg, n):
    return jax.ops.segment_sum(src, seg, n)
kernel_name = 'mk_gnn_resnorm_d1_gnn_r8_328efe'

def setup_inputs(seed: int=0):
    np.random.seed(seed)
    _w = jnp.asarray

    def _rec_inputs():
        import jax
        import jax.numpy as jnp
        _gk = jax.random.key(seed)
        x = -0.000202 + 1 * jax.random.normal(jax.random.fold_in(_gk, 1), (12500, 128), jnp.float32)
        src = jax.random.randint(jax.random.fold_in(_gk, 2), (400000,), 0, 12500, jnp.int32)
        dst = jax.random.randint(jax.random.fold_in(_gk, 3), (400000,), 0, 12500, jnp.int32)
        _o = jnp.argsort(dst, stable=True)
        src = src[_o]
        dst = dst[_o]
        edge_attr_64 = 0.000189758 + 1.00013 * jax.random.normal(jax.random.fold_in(_gk, 11), (400000, 64), jnp.float32)
        return (x, src, dst, edge_attr_64)
    x, src, dst, edge_attr_64 = _rec_inputs()

    def _L0_gnn_setup():
        import jax, jax.numpy as jnp
        import numpy as np
        N_NODES = 6250
        N_EDGES = 100000
        NODE_DIM = 128
        EDGE_DIM = 64
        HID = 64
        LN_EPS = 1e-05

        def _mlp2(h, W1, b1, W2, b2):
            return jax.nn.silu(h @ W1 + b1) @ W2 + b2
        key = jax.random.key(seed)
        ks = jax.random.split(key, 24)
        s = 0.05

        def rn(k, shape):
            return jax.random.normal(k, shape, dtype=jnp.float32) * s
        inp = {'x': jax.random.normal(ks[0], (N_NODES, NODE_DIM), dtype=jnp.float32), 'edge_index': jax.random.randint(ks[1], (2, N_EDGES), 0, N_NODES, dtype=jnp.int32), 'edge_attr': jax.random.normal(ks[2], (N_EDGES, EDGE_DIM), dtype=jnp.float32), 'node_W1': rn(ks[3], (NODE_DIM, HID)), 'node_b1': jnp.zeros((HID,), jnp.float32), 'node_W2': rn(ks[4], (HID, HID)), 'node_b2': jnp.zeros((HID,), jnp.float32), 'edge_W1': rn(ks[5], (EDGE_DIM, HID)), 'edge_b1': jnp.zeros((HID,), jnp.float32), 'edge_W2': rn(ks[6], (HID, HID)), 'edge_b2': jnp.zeros((HID,), jnp.float32), 'msg_W1': rn(ks[7], (3 * HID, HID)), 'msg_b1': jnp.zeros((HID,), jnp.float32), 'msg_W2': rn(ks[8], (HID, HID)), 'msg_b2': jnp.zeros((HID,), jnp.float32), 'upd_W1': rn(ks[9], (NODE_DIM + HID, HID)), 'upd_b1': jnp.zeros((HID,), jnp.float32), 'upd_W2': rn(ks[10], (HID, NODE_DIM)), 'upd_b2': jnp.zeros((NODE_DIM,), jnp.float32), 'ln_g': jnp.ones((NODE_DIM,), jnp.float32), 'ln_b': jnp.zeros((NODE_DIM,), jnp.float32)}
        return inp
    _L0_gnn_all = _L0_gnn_setup()
    _L0_gnn_in = {k: v for k, v in _L0_gnn_all.items() if k in ('node_W1', 'node_b1', 'node_W2', 'node_b2', 'edge_W1', 'edge_b1', 'edge_W2', 'edge_b2', 'msg_W1', 'msg_b1', 'msg_W2', 'msg_b2', 'upd_W1', 'upd_b1', 'upd_W2', 'upd_b2', 'ln_g', 'ln_b')}
    del _L0_gnn_all
    return {'x': x, 'src': src, 'dst': dst, 'edge_attr_64': edge_attr_64, 'L0_gnn_node_W1': _L0_gnn_in['node_W1'], 'L0_gnn_node_b1': _L0_gnn_in['node_b1'], 'L0_gnn_node_W2': _L0_gnn_in['node_W2'], 'L0_gnn_node_b2': _L0_gnn_in['node_b2'], 'L0_gnn_edge_W1': _L0_gnn_in['edge_W1'], 'L0_gnn_edge_b1': _L0_gnn_in['edge_b1'], 'L0_gnn_edge_W2': _L0_gnn_in['edge_W2'], 'L0_gnn_edge_b2': _L0_gnn_in['edge_b2'], 'L0_gnn_msg_W1': _L0_gnn_in['msg_W1'], 'L0_gnn_msg_b1': _L0_gnn_in['msg_b1'], 'L0_gnn_msg_W2': _L0_gnn_in['msg_W2'], 'L0_gnn_msg_b2': _L0_gnn_in['msg_b2'], 'L0_gnn_upd_W1': _L0_gnn_in['upd_W1'], 'L0_gnn_upd_b1': _L0_gnn_in['upd_b1'], 'L0_gnn_upd_W2': _L0_gnn_in['upd_W2'], 'L0_gnn_upd_b2': _L0_gnn_in['upd_b2'], 'L0_gnn_ln_g': _L0_gnn_in['ln_g'], 'L0_gnn_ln_b': _L0_gnn_in['ln_b']}

def reference(x, src, dst, edge_attr_64, L0_gnn_node_W1, L0_gnn_node_b1, L0_gnn_node_W2, L0_gnn_node_b2, L0_gnn_edge_W1, L0_gnn_edge_b1, L0_gnn_edge_W2, L0_gnn_edge_b2, L0_gnn_msg_W1, L0_gnn_msg_b1, L0_gnn_msg_W2, L0_gnn_msg_b2, L0_gnn_upd_W1, L0_gnn_upd_b1, L0_gnn_upd_W2, L0_gnn_upd_b2, L0_gnn_ln_g, L0_gnn_ln_b):
    import jax
    import jax.numpy as jnp

    def _L0_gnn_ref(x, edge_index, edge_attr, node_W1, node_b1, node_W2, node_b2, edge_W1, edge_b1, edge_W2, edge_b2, msg_W1, msg_b1, msg_W2, msg_b2, upd_W1, upd_b1, upd_W2, upd_b2, ln_g, ln_b):
        import jax, jax.numpy as jnp
        import numpy as np
        N_NODES = 6250
        N_EDGES = 100000
        NODE_DIM = 128
        EDGE_DIM = 64
        HID = 64
        LN_EPS = 1e-05

        def _mlp2(h, W1, b1, W2, b2):
            return jax.nn.silu(h @ W1 + b1) @ W2 + b2
        num_nodes = x.shape[0]
        src = edge_index[0]
        dst = edge_index[1]
        h_nodes = _mlp2(x, node_W1, node_b1, node_W2, node_b2)
        h_edges = _mlp2(edge_attr, edge_W1, edge_b1, edge_W2, edge_b2)
        msg_in = jnp.concatenate([h_nodes[dst], h_nodes[src], h_edges], axis=-1)
        msgs = _mlp2(msg_in, msg_W1, msg_b1, msg_W2, msg_b2)
        agg_sum = jax.ops.segment_sum(msgs, dst, num_segments=num_nodes)
        counts = jax.ops.segment_sum(jnp.ones((msgs.shape[0],), msgs.dtype), dst, num_segments=num_nodes)
        agg = agg_sum / jnp.maximum(counts, 1.0)[:, None]
        upd = _mlp2(jnp.concatenate([x, agg], axis=-1), upd_W1, upd_b1, upd_W2, upd_b2)
        out = x + upd
        mu = jnp.mean(out, axis=-1, keepdims=True)
        var = jnp.mean(jnp.square(out - mu), axis=-1, keepdims=True)
        out = (out - mu) * jax.lax.rsqrt(var + LN_EPS) * ln_g + ln_b
        return out
    edge_index = jnp.stack([src, dst])
    x = _layernorm(x + _L0_gnn_ref(x, edge_index, edge_attr_64, L0_gnn_node_W1, L0_gnn_node_b1, L0_gnn_node_W2, L0_gnn_node_b2, L0_gnn_edge_W1, L0_gnn_edge_b1, L0_gnn_edge_W2, L0_gnn_edge_b2, L0_gnn_msg_W1, L0_gnn_msg_b1, L0_gnn_msg_W2, L0_gnn_msg_b2, L0_gnn_upd_W1, L0_gnn_upd_b1, L0_gnn_upd_W2, L0_gnn_upd_b2, L0_gnn_ln_g, L0_gnn_ln_b), axis=-1)
    return x

_drawn_inputs = setup_inputs


def setup_inputs(seed=0):
    import zlib

    import numpy as np

    out = dict(_drawn_inputs(seed))
    spreads = {'L0_gnn_node_b1': (0.0, 2.0),
     'L0_gnn_node_b2': (0.0, 2.0),
     'L0_gnn_edge_b1': (0.0, 2.0),
     'L0_gnn_edge_b2': (0.0, 2.0),
     'L0_gnn_msg_b1': (0.0, 2.0),
     'L0_gnn_msg_b2': (0.0, 2.0),
     'L0_gnn_upd_b1': (0.0, 2.0),
     'L0_gnn_upd_b2': (0.0, 2.0),
     'L0_gnn_ln_g': (1.0, 0.2),
     'L0_gnn_ln_b': (0.0, 0.1)}
    factors = {'edge_attr_64': 8.0,
     'L0_gnn_node_W1': 8.0,
     'L0_gnn_node_W2': 8.0,
     'L0_gnn_edge_W1': 8.0,
     'L0_gnn_edge_W2': 8.0,
     'L0_gnn_msg_W1': 8.0,
     'L0_gnn_msg_W2': 8.0}
    for name, (base, spread) in spreads.items():
        noise = np.random.default_rng([zlib.crc32(name.encode()), seed]).standard_normal(out[name].shape)
        drawn = base * np.exp(spread * noise) if base else spread * noise
        out[name] = jnp.asarray(drawn.astype(out[name].dtype))
    for name, factor in factors.items():
        out[name] = (out[name] * factor).astype(out[name].dtype)
    return out
```

```python
import numpy as np
import concourse.bass as bass
import concourse.mybir as mybir
from contextlib import ExitStack

F32, BF16, I32 = mybir.dt.float32, mybir.dt.bfloat16, mybir.dt.int32
ALU, ACT, AX = mybir.AluOpType, mybir.ActivationFunctionType, mybir.AxisListType
ds = bass.ds

P = 128
H = 64
D = 128
W = 64
TILES = 5
UE = TILES * P
RING = 5
GN = 500
GJ = 4
GP = GN // GJ
EPS = 1e-5
BANK = 512


def build(nc, a, out):
    N = a["x"].shape[0]
    E = a["edgeT"].shape[1]
    UNITS = E // UE
    TURNS = UNITS // RING
    GROUPS = N // GN
    WINDOWS = -(-N // W)
    NPAD = N + W
    assert UNITS * UE == E and TURNS * RING == UNITS and TURNS > 1 and GROUPS * GN == N

    a_table = nc.dram_tensor("a_table", (NPAD, 3 * H), BF16, kind="Internal").ap()
    b_table = nc.dram_tensor("b_table", (N, H), F32, kind="Internal").ap()

    top = ExitStack()

    def pool_of(stack):
        def sb(name, shape, dt):
            return stack.enter_context(nc.sbuf_tensor(name, shape, dt))

        def ps(name, shape, dt=F32):
            return stack.enter_context(nc.psum_tensor(name, shape, dt))

        def sem(name):
            return stack.enter_context(nc.semaphore(name))
        return sb, ps, sem

    with top:
        sb, ps, sem = pool_of(top)
        agg = sb("agg", [P, NPAD], F32)
        dst_local = sb("dst_local", [P, E // P], F32)
        win_start = sb("win_start", [1, UNITS], I32)
        flag = sb("flag", [1, 1], I32)
        w_e1 = sb("w_e1", [H, H], F32)
        w_ef = sb("w_ef", [H, H], F32)
        b_e1 = sb("b_e1", [H, 1], F32)
        w_ux = sb("w_ux", [D, H], F32)
        w_ug = sb("w_ug", [H + 1, H], F32)
        b_u1 = sb("b_u1", [H, 1], F32)
        w_u2 = sb("w_u2", [H + 1, D], F32)
        ln_g = sb("ln_g", [P, D], F32)
        ln_b = sb("ln_b", [P, D], F32)
        iota = sb("iota", [P, W], F32)
        ident = sb("ident", [P, P], F32)

        tables(nc, a, pool_of, dict(locals()))
        with ExitStack() as stack:
            edges(nc, a, pool_of(stack), dict(locals()))
        update(nc, a, out, pool_of, dict(locals()))


def tables(nc, a, pool_of, v):
    N, E, UNITS, GROUPS, NPAD = v["N"], v["E"], v["UNITS"], v["GROUPS"], v["NPAD"]
    a_table, b_table, agg = v["a_table"], v["b_table"], v["agg"]
    dst_local, win_start, flag = v["dst_local"], v["win_start"], v["flag"]
    w_ef, w_ug, w_u2 = v["w_ef"], v["w_ug"], v["w_u2"]
    iota, ident = v["iota"], v["ident"]
    XR = 5
    SR = 2
    with ExitStack() as stack:
        sb, ps, sem = pool_of(stack)
        w_n1 = sb("w_n1", [D, H], F32)
        n2T = sb("n2T", [H, H], F32)
        e2T = sb("e2T", [H, H], F32)
        m2T = sb("m2T", [H, H], F32)
        wm1 = sb("wm1", [H, 3, H], F32)
        u1g = sb("u1g", [H, H], F32)
        b_n1 = sb("b_n1", [H, 1], F32)
        vecs = sb("vecs", [H, 3], F32)
        b_m1 = sb("b_m1", [1, H], F32)
        ones = sb("ones", [P, P], F32)
        w_ab = sb("w_ab", [H + 1, 2 * H], F32)
        xT = sb("xT", [D, XR, GN], F32)
        n1 = sb("n1", [H + 1, SR, GN], F32)
        ab = sb("ab", [GP, SR, GJ, 2 * H], F32)
        rest = sb("rest", [GP, SR, GJ, H], F32)
        parts = sb("parts", [GP, SR, GJ, 3, H], BF16)
        pad = sb("pad", [W, 3 * H], BF16)
        dst = sb("dst", [P, E // P], I32)
        startf = sb("startf", [1, UNITS], F32)
        spread = sb("spread", [P, 2], F32)
        bad = sb("bad", [P, 3], F32)
        p_w = ps("p_w", [P, BANK])
        p_b = ps("p_b", [P, BANK])
        p_h = ps("p_h", [H, 2, BANK])
        p_ab = ps("p_ab", [P, 2, BANK])
        p_s = ps("p_s", [P, 2, BANK])

        s_w = sem("weights_in")
        s_dst = sem("dst_in")
        s_x = [sem(f"x_in{i}") for i in range(XR)]
        s_const = sem("constants")
        s_iota = sem("pool_constants")
        s_fold = sem("folded")
        s_fcopy = sem("folded_copied")
        s_h = sem("hidden_psum")
        s_n1 = sem("hidden_done")
        s_ab = sem("ab_psum")
        s_abc = sem("ab_copied")
        s_hi = sem("hi_done")
        s_r1 = sem("rest1_done")
        s_mid = sem("mid_done")
        s_lo = sem("lo_done")
        s_st = [sem(f"ab_stored{i}") for i in range(SR)]
        s_pad = sem("pad_stored")
        s_sf = sem("start_float")
        s_sp = sem("start_spread")
        s_v = sem("vector_chain")
        s_bad = sem("bad_sum")
        block = stack.enter_context(nc.Block())
        spans = [(k, min(BANK, UNITS - k)) for k in range(0, UNITS, BANK)]
        assert len(spans) <= 2

        loads = [
            (w_n1[:, :], a["node_W1"]), (n2T[:, :], a["node_W2T"]), (e2T[:, :], a["edge_W2T"]),
            (m2T[:, :], a["msg_W2T"]), (wm1[:, :, :], a["msg_W1"].rearrange("(w k) n -> k w n", k=H)),
            (u1g[:, :], a["upd_W1"][D:D + H, :]), (v["w_ux"][:, :], a["upd_W1"][0:D, :]),
            (b_n1[:, :], a["node_b1"].unsqueeze(1)), (vecs[:, 0:1], a["node_b2"].unsqueeze(1)),
            (vecs[:, 1:2], a["edge_b2"].unsqueeze(1)), (vecs[:, 2:3], a["msg_b2"].unsqueeze(1)),
            (b_m1[:, :], a["msg_b1"].unsqueeze(0)), (v["w_e1"][:, :], a["edge_W1"]),
            (v["b_e1"][:, :], a["edge_b1"].unsqueeze(1)), (v["b_u1"][:, :], a["upd_b1"].unsqueeze(1)),
            (w_u2[0:H, :], a["upd_W2"]), (w_u2[H:H + 1, :], a["upd_b2"].unsqueeze(0)),
            (v["ln_g"][:, :], a["ln_g"].partition_broadcast(P)), (v["ln_b"][:, :], a["ln_b"].partition_broadcast(P)),
        ]

        def store(eng, g):
            rows = slice(g * GN, (g + 1) * GN)
            eng.wait_ge(s_abc, g + 1)
            eng.dma_start(b_table[rows, :].rearrange("(p j) n -> p j n", j=GJ), ab[:, g % SR, :, H:2 * H])\
               .then_inc(s_st[g % SR], 16)
            eng.wait_ge(s_lo, g + 1)
            eng.dma_start(a_table[rows, :].rearrange("(p j) n -> p (j n)", j=GJ),
                          parts[:, g % SR, :, :, :].rearrange("p j c n -> p (j c n)")).then_inc(s_st[g % SR], 16)

        def hidden(eng, g):
            eng.wait_ge(s_h, g + 1)
            if g >= SR:
                eng.wait_ge(s_ab, g - SR + 1)
            eng.activation(n1[0:H, g % SR, :], p_h[:, g % 2, 0:GN], ACT.Silu, bias=b_n1[:, :]).then_inc(s_n1, 1)

        def split(eng, g):
            s = g % SR
            eng.wait_ge(s_abc, g + 1)
            if g >= SR:
                eng.wait_ge(s_st[s], 32 * (g // SR))
            eng.copy(parts[:, s, :, 0, :], ab[:, s, :, 0:H]).then_inc(s_hi, 1)
            eng.wait_ge(s_r1, g + 1)
            eng.copy(parts[:, s, :, 1, :], rest[:, s, :, :]).then_inc(s_mid, 1)

        def hidden_mm(eng, g):
            eng.wait_ge(s_x[g % XR], 16 * (g // XR + 1))
            if g >= 2:
                eng.wait_ge(s_n1, g - 1)
            eng.matmul(p_h[:, g % 2, 0:GN], w_n1[:, :], xT[:, g % XR, :], start=True, stop=True).then_inc(s_h, 1)

        @block.sync
        def _(eng):
            for g in range(GROUPS):
                if g >= XR:
                    eng.wait_ge(s_h, g - XR + 1)
                eng.dma_start(xT[:, g % XR, :], a["xT"][:, g * GN:(g + 1) * GN]).then_inc(s_x[g % XR], 16)
                if g == 0:
                    eng.dma_start(dst[:, :], a["dst"]).then_inc(s_dst, 16)
                if g >= SR:
                    store(eng, g - SR)
            for g in range(GROUPS - SR, GROUPS):
                store(eng, g)
            for i in range(SR):
                eng.wait_ge(s_st[i], 32 * len(range(i, GROUPS, SR)))
            eng.wait_ge(s_pad, 16)

        @block.gpsimd
        def _(eng):
            eng.iota(iota[:, :], [[1, W]], base=0, channel_multiplier=0,
                     allow_small_or_imprecise_dtypes=True).then_inc(s_iota, 1)
            eng.memset(ident[:, :], 0.0).then_inc(s_iota, 1)
            eng.memset(pad[:, :], 0.0).then_inc(s_iota, 1)
            eng.wait_ge(s_iota, 3)
            eng.affine_select(out=ident[:, :], in_=ident[:, :], compare_op=ALU.not_equal, fill=1.0,
                              base=0, pattern=[[-1, P]], channel_multiplier=1).then_inc(s_iota, 1)
            eng.dma_start(a_table[N:NPAD, :], pad[:, :]).then_inc(s_pad, 16)
            for g in range(GROUPS):
                s = g % SR
                eng.wait_ge(s_hi, g + 1)
                eng.tensor_tensor(rest[:, s, :, :], ab[:, s, :, 0:H], parts[:, s, :, 0, :], ALU.subtract)\
                   .then_inc(s_r1, 1)
                eng.wait_ge(s_mid, g + 1)
                eng.tensor_tensor(parts[:, s, :, 2, :], rest[:, s, :, :], parts[:, s, :, 1, :], ALU.subtract)\
                   .then_inc(s_lo, 1)

        @block.scalar
        def _(eng):
            for to, of in loads:
                eng.dma_start(to, of).then_inc(s_w, 16)
            eng.wait_ge(s_w, 16 * len(loads))
            for g in range(GROUPS):
                hidden(eng, g)
                if g >= 1:
                    split(eng, g - 1)
            split(eng, GROUPS - 1)

        @block.tensor
        def _(eng):
            eng.wait_ge(s_w, 16 * len(loads))
            eng.wait_ge(s_const, 2)
            mm = eng.matmul
            mm(p_w[0:H, 0:2 * H], n2T[:, :], wm1[:, 0:2, :], start=True, stop=True)
            mm(p_w[0:H, 2 * H:3 * H], e2T[:, :], wm1[:, 2, :], start=True, stop=True)
            mm(p_w[0:H, 3 * H:4 * H], m2T[:, :], u1g[:, :], start=True, stop=True)
            row = p_b[H:H + 1, 0:H]
            mm(row, vecs[:, 0:1], wm1[:, 0, :], start=True, stop=False)
            mm(row, vecs[:, 0:1], wm1[:, 1, :], start=False, stop=False)
            mm(row, vecs[:, 1:2], wm1[:, 2, :], start=False, stop=False)
            mm(row, ones[0:1, 0:1], b_m1[:, :], start=False, stop=True)
            mm(p_b[H:H + 1, H:2 * H], vecs[:, 2:3], u1g[:, :], start=True, stop=True).then_inc(s_fold, 1)
            hidden_mm(eng, 0)
            for g in range(GROUPS):
                if g + 1 < GROUPS:
                    hidden_mm(eng, g + 1)
                eng.wait_ge(s_n1, g + 1)
                if g == 0:
                    eng.wait_ge(s_fcopy, 6)
                if g >= 2:
                    eng.wait_ge(s_abc, g - 1)
                for j in range(GJ):
                    last = mm(p_ab[0:GP, g % 2, j * 2 * H:(j + 1) * 2 * H], n1[:, g % SR, j:GN:GJ], w_ab[:, :],
                              start=True, stop=True)
                last.then_inc(s_ab, 1)
                if g == 1:
                    eng.wait_ge(s_sf, 1)
                    for n, (k, c) in enumerate(spans):
                        last = mm(p_s[:, n, 0:c], ones[0:1, :], startf[:, k:k + c], start=True, stop=True)
                    last.then_inc(s_sp, 1)
            eng.wait_ge(s_v, 6)
            mm(p_b[0:1, 256:257], bad[:, 2:3], ones[:, 0:1], start=True, stop=True).then_inc(s_bad, 1)

        @block.vector
        def _(eng):
            eng.memset(ones[:, :], 1.0).then_inc(s_const, 1)
            eng.memset(n1[H:H + 1, :, :], 1.0).then_inc(s_const, 1)
            eng.memset(w_ab[H:H + 1, H:2 * H], 0.0).then_inc(s_fcopy, 1)
            eng.memset(agg[:, :], 0.0)
            eng.wait_ge(s_fold, 1)
            eng.tensor_copy(w_ab[0:H, :], p_w[0:H, 0:2 * H]).then_inc(s_fcopy, 1)
            eng.tensor_copy(w_ab[H:H + 1, 0:H], p_b[H:H + 1, 0:H]).then_inc(s_fcopy, 1)
            eng.tensor_copy(w_ef[:, :], p_w[0:H, 2 * H:3 * H]).then_inc(s_fcopy, 1)
            eng.tensor_copy(w_ug[0:H, :], p_w[0:H, 3 * H:4 * H]).then_inc(s_fcopy, 1)
            eng.tensor_copy(w_ug[H:H + 1, :], p_b[H:H + 1, H:2 * H]).then_inc(s_fcopy, 1)

            def ab_copy(g):
                eng.wait_ge(s_ab, g + 1)
                if g >= SR:
                    eng.wait_ge(s_st[g % SR], 32 * (g // SR))
                eng.tensor_copy(ab[:, g % SR, :, :].rearrange("p j n -> p (j n)"), p_ab[0:GP, g % 2, :])\
                   .then_inc(s_abc, 1)

            for g in range(GROUPS):
                ab_copy(g)
                if g == 0:
                    eng.wait_ge(s_dst, 16)
                    first = dst[0:1, :].rearrange("p (u t) -> p u t", t=TILES)[:, :, 0]
                    eng.tensor_copy(win_start[:, :], first).then_inc(s_v, 1)
                    eng.tensor_copy(startf[:, :], first).then_inc(s_sf, 1)
                if g == 1:
                    eng.wait_ge(s_sp, 1)
                    for n, (k, c) in enumerate(spans):
                        view = lambda t: t[:, k * TILES:(k + c) * TILES].rearrange("p (u t) -> p u t", t=TILES)
                        last = eng.tensor_tensor(view(dst_local), view(dst),
                                                 p_s[:, n, 0:c].unsqueeze(2).to_broadcast([P, c, TILES]), ALU.subtract)
                    last.then_inc(s_v, 1)
            eng.wait_ge(s_v, 2)
            eng.tensor_reduce(spread[:, 0:1], dst_local[:, :], AX.X, ALU.max).then_inc(s_v, 1)
            eng.tensor_reduce(spread[:, 1:2], dst_local[:, :], AX.X, ALU.min).then_inc(s_v, 1)
            eng.wait_ge(s_v, 4)
            eng.tensor_scalar(bad[:, 0:1], spread[:, 0:1], float(W), None, ALU.is_ge)
            eng.tensor_scalar(bad[:, 1:2], spread[:, 1:2], 0.0, None, ALU.is_lt).then_inc(s_v, 1)
            eng.wait_ge(s_v, 5)
            eng.tensor_tensor(bad[:, 2:3], bad[:, 0:1], bad[:, 1:2], ALU.add).then_inc(s_v, 1)
            eng.wait_ge(s_bad, 1)
            eng.tensor_copy(flag[:, :], p_b[0:1, 256:257])


def edges(nc, a, tools, v):
    sb, ps, sem = tools
    E, N, UNITS, TURNS, WINDOWS = v["E"], v["N"], v["UNITS"], v["TURNS"], v["WINDOWS"]
    a_table, b_table, agg = v["a_table"], v["b_table"], v["agg"]
    dst_local, win_start, flag = v["dst_local"], v["win_start"], v["flag"]
    iota, ident = v["iota"], v["ident"]
    w_e1, w_ef, b_e1 = v["w_e1"], v["w_ef"], v["b_e1"]

    e_ring = sb("e_ring", [H, RING, UE], F32)
    src_ring = sb("src_ring", [P, RING, TILES], I32)
    b_ring = sb("b_ring", [P, RING, TILES, H], F32)
    a_ring = sb("a_ring", [W, RING, 3, H], BF16)
    hot_ring = sb("hot_ring", [P, RING, TILES, W], F32)
    hotT = sb("hotT", [W, UE], BF16)
    hid = sb("hid", [H, UE], F32)
    pre = sb("pre", [P, TILES, H], F32)
    msg = sb("msg", [P, TILES, 2 * H], F32)
    p_hid = ps("p_hid", [H, 2 * BANK])
    p_hot = ps("p_hot", [W, 2 * BANK])
    p_pre = ps("p_pre", [P, BANK])
    p_sum = ps("p_sum", [P, BANK])

    def ring_sems(name):
        return [sem(f"{name}{i}") for i in range(RING)]

    e_in, src_in, a_in, b_in = (ring_sems(n) for n in ("e_in", "src_in", "a_in", "b_in"))
    hid_mm = ring_sems("hid_mm")
    hid_ok = ring_sems("hid_ok")
    hot_ok = ring_sems("hot_ok")
    hotT_mm = ring_sems("hotT_mm")
    hotT_ok = ring_sems("hotT_ok")
    pre_mm = ring_sems("pre_mm")
    pre_ok = ring_sems("pre_ok")
    msg_ok = ring_sems("msg_ok")
    sum_mm = ring_sems("sum_mm")
    sum_ok = ring_sems("sum_ok")
    ones_ok = sem("ones_ok")
    marks = {str(e.engine): sem(f"mark{n}") for n, e in
             enumerate((nc.sync, nc.gpsimd, nc.tensor, nc.scalar, nc.vector))}
    gen = {n: sem("gen_" + n) for n in ("in", "b", "hid_mm", "hid", "pre_mm", "pre", "msg", "hot", "sum", "done", "v")}
    dst_raw = sb("dst_raw", [P, TILES], I32)
    dst_f = sb("dst_f", [P, TILES], F32)
    a_rows = sb("a_rows", [P, TILES, 3, H], BF16)
    iota_k = sb("iota_k", [P, W], F32)

    with nc.Block() as block:

        def wait_alone(eng, s, value):
            eng.wait_ge(s, value)
            eng.sem_inc(marks[str(eng.engine)], 1)

        def unit(turn, slot):
            return (turn + slot // RING, slot % RING)

        def col(u, width):
            return u[0] * (RING * width) + u[1] * width

        def turns(eng, body, ahead=0):
            with eng.Fori(0, TURNS - 1) as t:
                for slot in range(RING):
                    body(unit(t, slot), unit(t, slot + 1))
            for slot in range(RING):
                body(unit(TURNS - 1, slot), unit(TURNS - 1, slot + 1) if slot + 1 < RING else None)

        def choose(eng, fast, general):
            r = eng.value_load(flag[0:1, 0:1], min_val=0, max_val=2 * P)
            with eng.If(r == 0):
                fast(eng)
            with eng.Else():
                general(eng)

        def sync_fast(eng):
            def body(u, _):
                t, s = u
                eng.wait_ge(hid_mm[s], t + 1)
                eng.dma_start(e_ring[:, s, :], a["edgeT"][:, ds(col(u, UE), UE)]).then_inc(e_in[s], 16)
                eng.wait_ge(pre_ok[s], t + 1)
                eng.dma_start(src_ring[:, s, :], a["src"][:, ds(col(u, TILES), TILES)]).then_inc(src_in[s], 16)
                start = eng.value_load(win_start[0:1, ds(col(u, 1), 1)], min_val=0, max_val=N - 1)
                eng.dma_start(a_ring[:, s, :, :].rearrange("w c n -> w (c n)"), a_table[ds(start, W), :])\
                   .then_inc(a_in[s], 16)
            turns(eng, body)

        def pool_fast(eng):
            def body(u, _):
                t, s = u
                wait_alone(eng, src_in[s], 16 * t + 16)
                for k in range(TILES):
                    eng.indirect_dma_start(b_ring[:, s, k, :], None, b_table,
                                           bass.IndirectOffsetOnAxis(ap=src_ring[:, s, k:k + 1], axis=0))\
                       .then_inc(b_in[s], 16)
            turns(eng, body)

        def hidden_mm(eng, u):
            t, s = u
            wait_alone(eng, e_in[s], 16 * t + 16)
            for lo in range(0, UE, BANK):
                hi = min(UE, lo + BANK)
                last = eng.matmul(p_hid[:, lo:hi], w_e1[:, :], e_ring[:, s, lo:hi], start=True, stop=True)
            last.then_inc(hid_mm[s], 1)

        def hot_transpose(eng, u):
            t, s = u
            wait_alone(eng, hot_ok[s], t + 1)
            for k in range(TILES):
                last = eng.transpose(p_hot[:, k * P:(k + 1) * P], hot_ring[:, s, k, :], ident[:, :])
            last.then_inc(hotT_mm[s], 1)

        def tensor_fast(eng):
            def body(u, nxt):
                t, s = u
                eng.wait_ge(hid_ok[s], t + 1)
                eng.wait_ge(hotT_ok[s], t + 1)
                wait_alone(eng, a_in[s], 16 * t + 16)
                for k in range(TILES):
                    to = p_pre[:, k * H:(k + 1) * H]
                    eng.matmul(to, hid[:, k * P:(k + 1) * P], w_ef[:, :], start=True, stop=False)
                    for c in range(3):
                        last = eng.matmul(to, hotT[:, k * P:(k + 1) * P], a_ring[:, s, c, :],
                                          start=False, stop=c == 2)
                last.then_inc(pre_mm[s], 1)
                if nxt:
                    hidden_mm(eng, nxt)
                    hot_transpose(eng, nxt)
                eng.wait_ge(msg_ok[s], t + 1)
                eng.wait_ge(sum_ok[(s - 1) % RING], t + 1 if s == 0 else t + 2)
                for k in range(TILES):
                    last = eng.matmul(p_sum[:, 0:W], msg[:, k, :], hot_ring[:, s, k, :],
                                      start=k == 0, stop=k == TILES - 1)
                last.then_inc(sum_mm[s], 1)
            hidden_mm(eng, (0, 0))
            hot_transpose(eng, (0, 0))
            turns(eng, body)

        def scalar_front(eng, u):
            t, s = u
            eng.wait_ge(hid_mm[s], t + 2)
            eng.activation(hid[:, :], p_hid[:, 0:UE], ACT.Silu, bias=b_e1[:, :]).then_inc(hid_ok[s], 1)
            eng.wait_ge(hotT_mm[s], t + 1)
            eng.copy(hotT[:, :], p_hot[:, 0:UE]).then_inc(hotT_ok[s], 1)

        def scalar_fast(eng):
            def body(u, nxt):
                t, s = u
                eng.wait_ge(pre_ok[s], t + 2)
                eng.activation(msg[:, :, 0:H], pre[:, :, :], ACT.Silu).then_inc(msg_ok[s], 1)
                if nxt:
                    scalar_front(eng, nxt)
            scalar_front(eng, (0, 0))
            turns(eng, body)

        def one_hot(eng, u):
            t, s = u
            eng.tensor_tensor(hot_ring[:, s, :, :],
                              dst_local[:, ds(col(u, TILES), TILES)].unsqueeze(2).to_broadcast([P, TILES, W]),
                              iota[:, :].unsqueeze(1).to_broadcast([P, TILES, W]), ALU.is_equal).then_inc(hot_ok[s], 1)

        def vector_fast(eng):
            def body(u, nxt):
                t, s = u
                if nxt:
                    one_hot(eng, nxt)
                start = eng.value_load(win_start[0:1, ds(col(u, 1), 1)], min_val=0, max_val=N - 1)
                eng.wait_ge(pre_mm[s], t + 1)
                eng.wait_ge(b_in[s], 16 * TILES * t + 16 * TILES)
                eng.tensor_tensor(pre[:, :, :], p_pre[:, 0:TILES * H].rearrange("p (k n) -> p k n", n=H),
                                  b_ring[:, s, :, :], ALU.add).then_inc(pre_ok[s], 1)
                eng.wait_ge(sum_mm[s], t + 1)
                window = agg[:, ds(start, W)]
                wait_alone(eng, sum_ok[(s - 1) % RING], t + 1 if s == 0 else t + 2)
                eng.tensor_tensor(window, window, p_sum[:, 0:W], ALU.add).then_inc(sum_ok[s], 1)
            one_hot(eng, (0, 0))
            turns(eng, body)

        def sync_general(eng):
            with eng.Fori(0, UNITS) as u:
                wait_alone(eng, gen["done"], u + 1)
                eng.dma_start(e_ring[:, 0, :], a["edgeT"][:, ds(u * UE, UE)]).then_inc(gen["in"], 16)
                eng.dma_start(src_ring[:, 0, :], a["src"][:, ds(u * TILES, TILES)]).then_inc(gen["in"], 16)
                eng.dma_start(dst_raw[:, :], a["dst"][:, ds(u * TILES, TILES)]).then_inc(gen["in"], 16)

        def pool_general(eng):
            with eng.Fori(0, UNITS) as u:
                wait_alone(eng, gen["in"], 48 * u + 48)
                for k in range(TILES):
                    eng.indirect_dma_start(b_ring[:, 0, k, :], None, b_table,
                                           bass.IndirectOffsetOnAxis(ap=src_ring[:, 0, k:k + 1], axis=0))\
                       .then_inc(gen["b"], 16)
                    eng.indirect_dma_start(a_rows[:, k, :, :].rearrange("p c n -> p (c n)"), None, a_table,
                                           bass.IndirectOffsetOnAxis(ap=dst_raw[:, k:k + 1], axis=0))\
                       .then_inc(gen["b"], 16)

        def tensor_general(eng):
            with eng.Fori(0, UNITS) as u:
                wait_alone(eng, gen["in"], 48 * u + 48)
                for lo in range(0, UE, BANK):
                    hi = min(UE, lo + BANK)
                    last = eng.matmul(p_hid[:, lo:hi], w_e1[:, :], e_ring[:, 0, lo:hi], start=True, stop=True)
                last.then_inc(gen["hid_mm"], 1)
                wait_alone(eng, gen["hid"], u + 1)
                for k in range(TILES):
                    last = eng.matmul(p_pre[:, k * H:(k + 1) * H], hid[:, k * P:(k + 1) * P], w_ef[:, :],
                                      start=True, stop=True)
                last.then_inc(gen["pre_mm"], 1)
                wait_alone(eng, gen["msg"], u + 1)
                with eng.Fori(0, WINDOWS) as k:
                    wait_alone(eng, gen["hot"], u * WINDOWS + k + 1)
                    for n in range(TILES):
                        last = eng.matmul(p_sum[:, 0:W], msg[:, n, :], hot_ring[:, 0, n, :],
                                          start=n == 0, stop=n == TILES - 1)
                    last.then_inc(gen["sum"], 1)

        def scalar_general(eng):
            with eng.Fori(0, UNITS) as u:
                wait_alone(eng, gen["hid_mm"], u + 1)
                eng.activation(hid[:, :], p_hid[:, 0:UE], ACT.Silu, bias=b_e1[:, :]).then_inc(gen["hid"], 1)
                wait_alone(eng, gen["pre"], u + 1)
                eng.activation(msg[:, :, 0:H], pre[:, :, :], ACT.Silu).then_inc(gen["msg"], 1)

        def vector_general(eng):
            STEPS = 4 + 3
            with eng.Fori(0, UNITS) as u:
                links = u * (STEPS + 2 * WINDOWS)
                wait_alone(eng, gen["b"], 160 * u + 160)
                wait_alone(eng, gen["pre_mm"], u + 1)
                eng.tensor_tensor(pre[:, :, :], p_pre[:, 0:TILES * H].rearrange("p (k n) -> p k n", n=H),
                                  b_ring[:, 0, :, :], ALU.add).then_inc(gen["v"], 1)
                for c in range(3):
                    wait_alone(eng, gen["v"], links + 1 + c)
                    last = eng.tensor_tensor(pre[:, :, :], pre[:, :, :], a_rows[:, :, c, :], ALU.add)
                    last.then_inc(gen["v"] if c < 2 else gen["pre"], 1)
                eng.tensor_copy(dst_f[:, :], dst_raw[:, :]).then_inc(gen["v"], 1)
                eng.tensor_scalar(iota_k[:, :], iota[:, :], float(-W), None, ALU.add).then_inc(gen["v"], 1)
                wait_alone(eng, gen["v"], links + 5)
                with eng.Fori(0, WINDOWS) as k:
                    here = links + 5 + 2 * k
                    eng.tensor_scalar(iota_k[:, :], iota_k[:, :], float(W), None, ALU.add).then_inc(gen["v"], 1)
                    wait_alone(eng, gen["v"], here + 1)
                    eng.tensor_tensor(hot_ring[:, 0, :, :], dst_f[:, :].unsqueeze(2).to_broadcast([P, TILES, W]),
                                      iota_k[:, :].unsqueeze(1).to_broadcast([P, TILES, W]), ALU.is_equal)\
                       .then_inc(gen["hot"], 1)
                    wait_alone(eng, gen["sum"], u * WINDOWS + k + 1)
                    window = agg[:, ds(k * W, W)]
                    eng.tensor_tensor(window, window, p_sum[:, 0:W], ALU.add).then_inc(gen["v"], 1)
                    wait_alone(eng, gen["v"], here + 2)
                eng.tensor_copy(dst_f[:, 0:1], dst_f[:, 1:2]).then_inc(gen["v"], 1)
                eng.sem_inc(gen["v"], 1)
                wait_alone(eng, gen["v"], links + STEPS + 2 * WINDOWS)
                eng.sem_inc(gen["done"], 1)

        @block.sync
        def _(eng):
            choose(eng, sync_fast, sync_general)

        @block.gpsimd
        def _(eng):
            choose(eng, pool_fast, pool_general)

        @block.tensor
        def _(eng):
            for s in range(RING):
                eng.sem_inc(hid_mm[s], 1)
            eng.wait_ge(ones_ok, 1)
            choose(eng, tensor_fast, tensor_general)

        @block.scalar
        def _(eng):
            choose(eng, scalar_fast, scalar_general)

        @block.vector
        def _(eng):
            for s in range(RING):
                eng.sem_inc(pre_ok[s], 1)
                eng.sem_inc(sum_ok[s], 1)
            eng.sem_inc(gen["done"], 1)
            eng.memset(msg[:, :, H:2 * H], 1.0).then_inc(ones_ok, 1)
            choose(eng, vector_fast, vector_general)


def update(nc, a, out, pool_of, v):
    GROUPS = v["GROUPS"]
    agg, w_ux, w_ug, b_u1, w_u2 = v["agg"], v["w_ux"], v["w_ug"], v["b_u1"], v["w_u2"]
    ln_g, ln_b = v["ln_g"], v["ln_b"]
    R = 4
    with ExitStack() as stack:
        sb, ps, sem = pool_of(stack)
        xT = sb("u_xT", [D, R, GN], F32)
        x = sb("u_x", [GP, R, GJ, D], F32)
        inv = sb("u_inv", [H, R, GN], F32)
        hid = sb("u_hid", [H + 1, R, GN], F32)
        y = sb("u_y", [GP, R, GJ, D], F32)
        z = sb("u_z", [GP, R, GJ, D], F32)
        o = sb("u_o", [GP, R, GJ, D], F32)
        stats = sb("u_stats", [GP, R, GJ, 6], F32)
        mv = sb("u_mv", [GP, R, 2, GJ, 2], F32)
        rstd = sb("u_rstd", [GP, R, 2, GJ], F32)
        shift = sb("u_shift", [GP, R, 2, GJ], F32)
        power = sb("u_power", [GP, GJ], F32)
        p_u = ps("p_u", [H, 2, BANK])
        p_d = ps("p_d", [P, 2, BANK])
        s_in = [sem(f"x_in{i}") for i in range(R)]
        s_out = [sem(f"out{i}") for i in range(R)]
        s_c = sem("constants")
        s_mean = sem("mean")
        s_u = sem("u_psum")
        s_h = sem("u_hidden")
        s_d = sem("d_psum")
        s_mv = sem("moments")
        s_rs = sem("rstd")
        s_z = sem("normed1")
        s_zg = sem("scaled")
        s_r2 = sem("residual2")
        s_o = sem("normed2")
        s_y = sem("y_sum")
        s_p = sem("pool_chain")
        s_v = sem("vector_chain")
        block = stack.enter_context(nc.Block())

        def moment(g, k):
            if k == 0:
                return 1 if g == 0 else 2 * g
            return 2 * g + 3 if g + 1 < GROUPS else 2 * GROUPS

        def rows(t, g):
            return t[g * GN:(g + 1) * GN, :].rearrange("(p j) n -> p j n", j=GJ)

        @block.sync
        def _(eng):
            for g in range(GROUPS + R):
                if g < GROUPS:
                    r = g % R
                    if g >= R:
                        eng.wait_ge(s_u, g - R + 1)
                        eng.wait_ge(s_r2, g - R + 1)
                    eng.dma_start(xT[:, r, :], a["xT"][:, g * GN:(g + 1) * GN]).then_inc(s_in[r], 16)
                    eng.dma_start(x[:, r, :, :], rows(a["x"], g)).then_inc(s_in[r], 16)

        @block.gpsimd
        def _(eng):
            eng.memset(power[:, :], -0.5).then_inc(s_c, 1)
            eng.wait_ge(s_c, 3)
            chain = 0
            for n in range(GROUPS + 1):
                for g, k in ((n, 0), (n - 1, 1)):
                    if not 0 <= g < GROUPS:
                        continue
                    r = g % R
                    eng.wait_ge(s_mv, moment(g, k))
                    eng.tensor_scalar(rstd[:, r, k, :], mv[:, r, k, :, 1], EPS, None, ALU.add).then_inc(s_p, 1)
                    chain += 1
                    eng.wait_ge(s_p, chain)
                    eng.tensor_tensor(rstd[:, r, k, :], rstd[:, r, k, :], power[:, :], ALU.pow).then_inc(s_p, 1)
                    chain += 1
                    eng.wait_ge(s_p, chain)
                    eng.tensor_tensor(shift[:, r, k, :], mv[:, r, k, :, 0], rstd[:, r, k, :], ALU.mult).then_inc(s_p, 1)
                    chain += 1
                    eng.wait_ge(s_p, chain)
                    eng.tensor_scalar(shift[:, r, k, :], shift[:, r, k, :], -1.0, None, ALU.mult).then_inc(s_rs, 1)
                    if k == 0:
                        eng.wait_ge(s_z, g + 1)
                        wide = [GP, GJ, D]
                        eng.tensor_tensor(z[:, r, :, :], z[:, r, :, :], ln_g[0:GP, :].unsqueeze(1).to_broadcast(wide),
                                          ALU.mult).then_inc(s_p, 1)
                        chain += 1
                        eng.wait_ge(s_p, chain)
                        eng.tensor_tensor(z[:, r, :, :], z[:, r, :, :], x[:, r, :, :], ALU.add).then_inc(s_r2, 1)

        @block.scalar
        def _(eng):
            def hidden(g):
                eng.wait_ge(s_u, g + 1)
                if g >= R:
                    eng.wait_ge(s_d, g - R + 1)
                eng.activation(hid[0:H, g % R, :], p_u[:, g % 2, 0:GN], ACT.Silu, bias=b_u1[:, :]).then_inc(s_h, 1)

            def norm(g, k, to, of, done):
                eng.wait_ge(s_rs, moment(g, k))
                if k == 1 and g >= R:
                    eng.wait_ge(s_out[g % R], 16 * (g // R))
                for j in range(GJ):
                    last = eng.activation(to[:, g % R, j, :], of[:, g % R, j, :], ACT.Identity,
                                          bias=shift[:, g % R, k, j:j + 1], scale=rstd[:, g % R, k, j:j + 1])
                last.then_inc(done, 1)

            eng.wait_ge(s_c, 3)
            hidden(0)
            for g in range(GROUPS + 1):
                if g + 1 < GROUPS:
                    hidden(g + 1)
                if g < GROUPS:
                    norm(g, 0, z, y, s_z)
                if g >= 1:
                    norm(g - 1, 1, o, y, s_o)
                    eng.wait_ge(s_o, g)
                    eng.dma_start(rows(out, g - 1), o[:, (g - 1) % R, :, :]).then_inc(s_out[(g - 1) % R], 16)
            for r in range(R):
                eng.wait_ge(s_out[r], 16 * len(range(r, GROUPS, R)))

        @block.tensor
        def _(eng):
            def up(g):
                r = g % R
                eng.wait_ge(s_in[r], 32 * (g // R + 1))
                eng.wait_ge(s_mean, g + 1)
                if g >= 2:
                    eng.wait_ge(s_h, g - 1)
                eng.matmul(p_u[:, g % 2, 0:GN], w_ux[:, :], xT[:, r, :], start=True, stop=False)
                eng.matmul(p_u[:, g % 2, 0:GN], w_ug[:, :], agg[0:H + 1, g * GN:(g + 1) * GN], start=False, stop=True)\
                   .then_inc(s_u, 1)

            eng.wait_ge(s_c, 3)
            up(0)
            for g in range(GROUPS):
                if g + 1 < GROUPS:
                    up(g + 1)
                eng.wait_ge(s_h, g + 1)
                if g >= 2:
                    eng.wait_ge(s_y, g - 1)
                for j in range(GJ):
                    last = eng.matmul(p_d[0:GP, g % 2, j * D:(j + 1) * D], hid[:, g % R, j:GN:GJ], w_u2[:, :],
                                      start=True, stop=True)
                last.then_inc(s_d, 1)

        @block.vector
        def _(eng):
            eng.memset(hid[H:H + 1, :, :], 1.0).then_inc(s_c, 2)
            links = [0]

            def link(ins):
                links[0] += 1
                ins.then_inc(s_v, 1)
                eng.wait_ge(s_v, links[0])

            def mean(g):
                cols = slice(g * GN, (g + 1) * GN)
                r = g % R
                link(eng.tensor_scalar(inv[:, r, :], agg[H:2 * H, cols], 1.0, None, ALU.max))
                eng.tensor_scalar(agg[H:H + 1, cols], agg[H:H + 1, cols], 1.0, None, ALU.min)
                link(eng.reciprocal(inv[:, r, :], inv[:, r, :]))
                eng.tensor_tensor(agg[0:H, cols], agg[0:H, cols], inv[:, r, :], ALU.mult).then_inc(s_mean, 1)

            def moments(g, k):
                r = g % R
                for j in range(GJ):
                    last = eng.bn_stats(stats[:, r, j, :], y[:, r, j, :])
                link(last)
                for j in range(GJ):
                    last = eng.bn_aggr(mv[:, r, k, j, :], stats[:, r, j, :])
                last.then_inc(s_mv, 1)

            mean(0)
            for g in range(GROUPS + 1):
                if g + 1 < GROUPS:
                    mean(g + 1)
                if g < GROUPS:
                    r = g % R
                    eng.wait_ge(s_d, g + 1)
                    eng.wait_ge(s_in[r], 32 * (g // R + 1))
                    if g >= R:
                        eng.wait_ge(s_o, g - R + 1)
                    eng.tensor_tensor(y[:, r, :, :], p_d[0:GP, g % 2, :].rearrange("p (j n) -> p j n", n=D),
                                      x[:, r, :, :], ALU.add).then_inc(s_y, 1)
                    eng.wait_ge(s_y, g + 1)
                    moments(g, 0)
                if g >= 1:
                    r = (g - 1) % R
                    eng.wait_ge(s_r2, g)
                    link(eng.tensor_tensor(y[:, r, :, :], z[:, r, :, :],
                                           ln_b[0:GP, :].unsqueeze(1).to_broadcast([GP, GJ, D]), ALU.add))
                    moments(g - 1, 1)


def _laid_out(inputs):
    g = {k.removeprefix("L0_gnn_"): np.asarray(t) for k, t in inputs.items()}
    keep = ["x", "node_W1", "node_b1", "node_b2", "edge_W1", "edge_b1", "edge_b2", "msg_W1", "msg_b1", "msg_b2",
            "upd_W1", "upd_b1", "upd_W2", "upd_b2", "ln_g", "ln_b"]
    d = {k: g[k] for k in keep}
    d["xT"] = g["x"].T
    d["edgeT"] = g["edge_attr_64"].T
    for k in ("node_W2", "edge_W2", "msg_W2"):
        d[k + "T"] = g[k].T
    for k in ("src", "dst"):
        d[k] = g[k].reshape(-1, P).T
    return {k: np.ascontiguousarray(t) for k, t in d.items()}


def kernel(**inputs):
    import concourse.bacc as bacc
    from concourse.bass_utils import run_bass_kernel_spmd

    nc = bacc.Bacc("TRN2", target_bir_lowering=False, num_devices=1)
    arrays = {f"in_{k}": t for k, t in _laid_out(inputs).items()}
    aps = {k[3:]: nc.dram_tensor(k, t.shape, mybir.dt.from_np(t.dtype), kind="ExternalInput").ap()
           for k, t in arrays.items()}
    out = nc.dram_tensor("out", inputs["x"].shape, F32, kind="ExternalOutput").ap()
    build(nc, aps, out)
    r = run_bass_kernel_spmd(nc, [arrays], core_ids=[0])
    return r.results[0]["out"]
```

```python
import numpy as np
import concourse.bass as bass
import concourse.mybir as mybir
from contextlib import ExitStack

F32, BF16, I32 = mybir.dt.float32, mybir.dt.bfloat16, mybir.dt.int32
ALU, ACT, AX = mybir.AluOpType, mybir.ActivationFunctionType, mybir.AxisListType
ds = bass.ds

P = 128
H = 64
D = 128
W = 64
TILES = 5
UE = TILES * P
RING = 5
GN = 500
GJ = 4
GP = GN // GJ
PAIRS = -(-TILES // 2)
PAIR_COLS = [2 * H] * (TILES // 2) + [H] * (TILES % 2)
ECOLS = PAIRS * P
ELOW = UE - ECOLS
ORDER = [k // 2 + (PAIRS if k % 2 else 0) for k in range(TILES)]
EPS = 1e-5
BANK = 512


def build(nc, a, out):
    N = a["x"].shape[0]
    E = a["edgeT"].shape[1]
    UNITS = E // UE
    TURNS = UNITS // RING
    GROUPS = N // GN
    WINDOWS = -(-N // W)
    NPAD = N + W
    assert UNITS * UE == E and TURNS * RING == UNITS and TURNS > 1 and GROUPS * GN == N

    a_table = nc.dram_tensor("a_table", (NPAD, 3 * H), BF16, kind="Internal").ap()
    b_table = nc.dram_tensor("b_table", (N, H), F32, kind="Internal").ap()

    with ExitStack() as top:
        sb = tools(nc, top)[0]
        agg = sb("agg", [P, NPAD], F32)
        w_ux = sb("w_ux", [D, H], F32)
        w_ug = sb("w_ug", [H + 1, H], F32)
        b_u1 = sb("b_u1", [H, 1], F32)
        w_u2 = sb("w_u2", [H + 1, D], F32)
        ln_g = sb("ln_g", [P, D], F32)
        ln_b = sb("ln_b", [P, D], F32)
        v = dict(locals())
        with ExitStack() as stack:
            messages(nc, a, stack, v)
        with ExitStack() as stack:
            update(nc, a, out, stack, v)


def tools(nc, stack):
    def sb(name, shape, dt):
        return stack.enter_context(nc.sbuf_tensor(name, shape, dt))

    def ps(name, shape, dt=F32):
        return stack.enter_context(nc.psum_tensor(name, shape, dt))

    def sem(name):
        return stack.enter_context(nc.semaphore(name))
    return sb, ps, sem


def messages(nc, a, stack, v):
    sb, ps, sem = tools(nc, stack)
    E, N, UNITS, TURNS, GROUPS = v["E"], v["N"], v["UNITS"], v["TURNS"], v["GROUPS"]
    WINDOWS, NPAD = v["WINDOWS"], v["NPAD"]
    a_table, b_table, agg = v["a_table"], v["b_table"], v["agg"]
    w_ug, w_u2 = v["w_ug"], v["w_u2"]

    dst_local = sb("dst_local", [P, E // P], F32)
    win_start = sb("win_start", [1, UNITS], I32)
    flag = sb("flag", [1, 1], I32)
    iota = sb("iota", [P, W], F32)
    ident = sb("ident", [P, P], F32)
    w_e1 = sb("w_e1", [P, P], F32)
    w_ef = sb("w_ef", [P, P], F32)
    b_e1 = sb("b_e1", [P, 1], F32)
    w_n1 = sb("w_n1", [D, H], F32)
    n2T = sb("n2T", [H, H], F32)
    e2T = sb("e2T", [H, H], F32)
    m2T = sb("m2T", [H, H], F32)
    wm1 = sb("wm1", [H, 3, H], F32)
    u1g = sb("u1g", [H, H], F32)
    b_n1 = sb("b_n1", [H, 1], F32)
    vecs = sb("vecs", [H, 3], F32)
    b_m1 = sb("b_m1", [1, H], F32)
    ones = sb("ones", [P, P], F32)
    w_ab = sb("w_ab", [H + 1, 2 * H], F32)

    XR = 6
    SR = 4
    xT = sb("xT", [D, XR, GN], F32)
    n1 = sb("n1", [H + 1, SR, GN], F32)
    ab = sb("ab", [GP, SR, GJ, 2 * H], F32)
    rest = sb("rest", [GP, SR, GJ, H], F32)
    parts = sb("parts", [GP, SR, GJ, 3, H], BF16)
    pad = sb("pad", [W, 3 * H], BF16)
    dst = sb("dst", [P, E // P], I32)
    startf = sb("startf", [1, UNITS], F32)
    spread = sb("spread", [P, 2], F32)
    bad = sb("bad", [P, 3], F32)

    e_ring = sb("e_ring", [P, RING, ECOLS], F32)
    src_ring = sb("src_ring", [P, RING, TILES], I32)
    b_ring = sb("b_ring", [P, RING, TILES, H], F32)
    a_ring = sb("a_ring", [P, RING, 3, 2 * H], BF16)
    hot_ring = sb("hot_ring", [P, RING, TILES + 1, W], F32)
    hotT = sb("hotT", [P, ECOLS], BF16)
    hid = sb("hid", [P, ECOLS], F32)
    pre = sb("pre", [P, TILES, H], F32)
    msg = sb("msg", [P, TILES, 2 * H], F32)
    dst_raw = sb("dst_raw", [P, TILES], I32)
    dst_f = sb("dst_f", [P, TILES], F32)
    a_rows = sb("a_rows", [P, TILES, 3, H], BF16)
    iota_k = sb("iota_k", [P, W], F32)

    p_hid = ps("p_hid", [P, BANK])
    p_hot = ps("p_hot", [P, BANK])
    p_pre = ps("p_pre", [P, BANK])
    p_sum = ps("p_sum", [P, BANK])
    p_h = ps("p_h", [H, 2, BANK])
    p_ab = ps("p_ab", [P, 2, BANK])
    p_w, p_b = p_hid, p_hot
    spans = [(k, min(BANK, UNITS - k), bank) for k, bank in zip(range(0, UNITS, BANK), (p_pre, p_sum))]
    assert spans[-1][0] + spans[-1][1] == UNITS

    s_w = sem("weights_in")
    s_dst = sem("dst_in")
    s_x = [sem(f"x_in{i}") for i in range(XR)]
    s_const = sem("constants")
    s_pool = sem("pool_constants")
    s_fold = sem("folded")
    s_fcopy = sem("folded_copied")
    s_h = sem("hidden_psum")
    s_n1 = sem("hidden_done")
    s_ab = sem("ab_psum")
    s_abc = sem("ab_copied")
    s_hi = sem("hi_done")
    s_r1 = sem("rest_done")
    s_mid = sem("mid_done")
    s_lo = sem("lo_done")
    s_sta = [sem(f"a_stored{i}") for i in range(SR)]
    s_stb = [sem(f"b_stored{i}") for i in range(SR)]
    s_pad = sem("pad_stored")
    s_sf = sem("start_float")
    s_sp = sem("start_spread")
    s_v = sem("vector_chain")
    s_bad = sem("bad_sum")
    s_flag = sem("flag_done")

    def ring_sems(name):
        return [sem(f"{name}{i}") for i in range(RING)]

    ea_in, eb_in, src_in, a_in, b_in = (ring_sems(n) for n in ("ea_in", "eb_in", "src_in", "a_in", "b_in"))
    hid_mm = ring_sems("hid_mm")
    hid_ok = ring_sems("hid_ok")
    hot_ok = ring_sems("hot_ok")
    hotT_mm = ring_sems("hotT_mm")
    hotT_ok = ring_sems("hotT_ok")
    pre_mm = ring_sems("pre_mm")
    pre_ok = ring_sems("pre_ok")
    msg_ok = ring_sems("msg_ok")
    sum_mm = ring_sems("sum_mm")
    sum_ok = ring_sems("sum_ok")
    marks = {str(e.engine): sem(f"mark{n}") for n, e in enumerate((nc.sync, nc.gpsimd, nc.tensor, nc.scalar, nc.vector))}
    gen = {n: sem("gen_" + n) for n in ("in", "b", "hid_mm", "hid", "pre_mm", "pre", "msg", "hot", "sum", "done", "v")}

    loads = [
        (w_n1[:, :], a["node_W1"]), (n2T[:, :], a["node_W2T"]), (wm1[:, :, :], a["msg_W1"].rearrange("(w k) n -> k w n", k=H)),
        (e2T[:, :], a["edge_W2T"]), (m2T[:, :], a["msg_W2T"]), (u1g[:, :], a["upd_W1"][D:D + H, :]),
        (b_n1[:, :], a["node_b1"].unsqueeze(1)), (vecs[:, 0:1], a["node_b2"].unsqueeze(1)),
        (vecs[:, 1:2], a["edge_b2"].unsqueeze(1)), (vecs[:, 2:3], a["msg_b2"].unsqueeze(1)),
        (b_m1[:, :], a["msg_b1"].unsqueeze(0)),
    ]
    later_loads = [
        (w_e1[0:H, 0:H], a["edge_W1"]), (w_e1[H:P, H:P], a["edge_W1"]),
        (b_e1[0:H, :], a["edge_b1"].unsqueeze(1)), (b_e1[H:P, :], a["edge_b1"].unsqueeze(1)),
        (v["w_ux"][:, :], a["upd_W1"][0:D, :]), (v["b_u1"][:, :], a["upd_b1"].unsqueeze(1)),
        (w_u2[0:H, :], a["upd_W2"]), (w_u2[H:H + 1, :], a["upd_b2"].unsqueeze(0)),
        (v["ln_g"][:, :], a["ln_g"].partition_broadcast(P)), (v["ln_b"][:, :], a["ln_b"].partition_broadcast(P)),
    ]
    s_w2 = sem("later_weights_in")

    def sync_nodes(eng):
        LAG = SR + 1
        for g in range(GROUPS + LAG):
            if g < GROUPS:
                if g >= XR:
                    eng.wait_ge(s_h, g - XR + 1)
                eng.dma_start(xT[:, g % XR, :], a["xT"][:, g * GN:(g + 1) * GN]).then_inc(s_x[g % XR], 16)
            if g == 1:
                eng.dma_start(dst[:, :], a["dst"]).then_inc(s_dst, 16)
            if g >= LAG:
                k = g - LAG
                eng.wait_ge(s_lo, k + 1)
                eng.dma_start(a_table[k * GN:(k + 1) * GN, :].rearrange("(p j) n -> p (j n)", j=GJ),
                              parts[:, k % SR, :, :, :].rearrange("p j c n -> p (j c n)")).then_inc(s_sta[k % SR], 16)

    def sync_tables_done(eng):
        for i in range(SR):
            eng.wait_ge(s_sta[i], 16 * len(range(i, GROUPS, SR)))
        eng.wait_ge(s_pad, 16)

    def pool_nodes(eng):
        eng.iota(iota[:, :], [[1, W]], base=0, channel_multiplier=0,
                 allow_small_or_imprecise_dtypes=True).then_inc(s_pool, 1)
        eng.memset(ident[:, :], 0.0).then_inc(s_pool, 1)
        eng.memset(pad[:, :], 0.0).then_inc(s_pool, 1)
        eng.memset(a_ring[:, :, :, :], 0.0).then_inc(s_pool, 1)
        eng.wait_ge(s_pool, 4)
        eng.memset(e_ring[H:P, :, ELOW:ECOLS], 0.0).then_inc(s_pool, 1)
        eng.wait_ge(s_pool, 5)
        eng.memset(hot_ring[:, :, TILES, :], 0.0).then_inc(s_pool, 1)
        eng.wait_ge(s_pool, 6)
        eng.affine_select(out=ident[:, :], in_=ident[:, :], compare_op=ALU.not_equal, fill=1.0,
                          base=0, pattern=[[-1, P]], channel_multiplier=1).then_inc(s_pool, 1)
        eng.dma_start(a_table[N:NPAD, :], pad[:, :]).then_inc(s_pad, 16)
        for g in range(GROUPS):
            eng.wait_ge(s_abc, g + 1)
            eng.dma_start(b_table[g * GN:(g + 1) * GN, :].rearrange("(p j) n -> p j n", j=GJ),
                          ab[:, g % SR, :, H:2 * H]).then_inc(s_stb[g % SR], 16)
        for i in range(SR):
            eng.wait_ge(s_stb[i], 16 * len(range(i, GROUPS, SR)))

    def scalar_nodes(eng):
        for to, of in loads:
            eng.dma_start(to, of).then_inc(s_w, 16)
        eng.wait_ge(s_w, 16 * len(loads))
        for g in range(GROUPS + 2):
            if g < GROUPS:
                eng.wait_ge(s_h, g + 1)
                if g >= SR:
                    eng.wait_ge(s_ab, g - SR + 1)
                eng.activation(n1[0:H, g % SR, :], p_h[:, g % 2, 0:GN], ACT.Silu, bias=b_n1[:, :]).then_inc(s_n1, 1)
            if 1 <= g <= GROUPS:
                k = g - 1
                eng.wait_ge(s_abc, k + 1)
                if k >= SR:
                    eng.wait_ge(s_sta[k % SR], 16 * (k // SR))
                eng.copy(parts[:, k % SR, :, 0, :], ab[:, k % SR, :, 0:H]).then_inc(s_hi, 1)
            if g >= 2:
                k = g - 2
                eng.wait_ge(s_r1, k + 1)
                eng.copy(parts[:, k % SR, :, 1, :], rest[:, k % SR, :, :]).then_inc(s_mid, 1)
            if g == 2:
                for to, of in later_loads:
                    eng.dma_start(to, of).then_inc(s_w2, 16)

    def tensor_nodes(eng):
        eng.wait_ge(s_w, 16 * len(loads))
        eng.wait_ge(s_const, 2)
        mm = eng.matmul

        def node_hidden(g):
            eng.wait_ge(s_x[g % XR], 16 * (g // XR + 1))
            if g >= 2:
                eng.wait_ge(s_n1, g - 1)
            mm(p_h[:, g % 2, 0:GN], w_n1[:, :], xT[:, g % XR, :], start=True, stop=True).then_inc(s_h, 1)

        mm(p_w[0:H, 0:2 * H], n2T[:, :], wm1[:, 0:2, :], start=True, stop=True)
        mm(p_w[0:H, 2 * H:3 * H], e2T[:, :], wm1[:, 2, :], start=True, stop=True)
        mm(p_w[0:H, 3 * H:4 * H], m2T[:, :], u1g[:, :], start=True, stop=True)
        row = p_b[H:H + 1, 0:H]
        mm(row, vecs[:, 0:1], wm1[:, 0, :], start=True, stop=False)
        mm(row, vecs[:, 0:1], wm1[:, 1, :], start=False, stop=False)
        mm(row, vecs[:, 1:2], wm1[:, 2, :], start=False, stop=False)
        mm(row, ones[0:1, 0:1], b_m1[:, :], start=False, stop=True)
        mm(p_b[H:H + 1, H:2 * H], vecs[:, 2:3], u1g[:, :], start=True, stop=True).then_inc(s_fold, 1)
        node_hidden(0)
        for g in range(GROUPS):
            if g + 1 < GROUPS:
                node_hidden(g + 1)
            eng.wait_ge(s_n1, g + 1)
            if g == 0:
                eng.wait_ge(s_fcopy, 7)
            if g >= 2:
                eng.wait_ge(s_abc, g - 1)
            for j in range(GJ):
                last = mm(p_ab[0:GP, g % 2, j * 2 * H:(j + 1) * 2 * H], n1[:, g % SR, j:GN:GJ], w_ab[:, :],
                          start=True, stop=True)
            last.then_inc(s_ab, 1)
            if g == 1:
                eng.wait_ge(s_sf, 1)
                for k, c, bank in spans:
                    last = mm(bank[:, 0:c], ones[0:1, :], startf[:, k:k + c], start=True, stop=True)
                last.then_inc(s_sp, 1)
        eng.wait_ge(s_v, 6)
        mm(p_b[0:1, 256:257], bad[:, 2:3], ones[:, 0:1], start=True, stop=True).then_inc(s_bad, 1)

    def vector_nodes(eng):
        eng.memset(ones[:, :], 1.0).then_inc(s_const, 1)
        eng.memset(n1[H:H + 1, :, :], 1.0).then_inc(s_const, 1)
        for t in (w_ef, w_e1):
            eng.memset(t[0:H, H:P], 0.0)
            eng.memset(t[H:P, 0:H], 0.0)
        eng.memset(w_ab[H:H + 1, H:2 * H], 0.0).then_inc(s_fcopy, 1)
        eng.memset(agg[:, :], 0.0).then_inc(s_const, 1)
        eng.memset(msg[:, :, H:2 * H], 1.0).then_inc(s_const, 1)
        eng.wait_ge(s_fold, 1)
        eng.tensor_copy(w_ab[0:H, :], p_w[0:H, 0:2 * H]).then_inc(s_fcopy, 1)
        eng.tensor_copy(w_ab[H:H + 1, 0:H], p_b[H:H + 1, 0:H]).then_inc(s_fcopy, 1)
        eng.tensor_copy(w_ef[0:H, 0:H], p_w[0:H, 2 * H:3 * H]).then_inc(s_fcopy, 1)
        eng.tensor_copy(w_ef[H:P, H:P], p_w[0:H, 2 * H:3 * H]).then_inc(s_fcopy, 1)
        eng.tensor_copy(w_ug[0:H, :], p_w[0:H, 3 * H:4 * H]).then_inc(s_fcopy, 1)
        eng.tensor_copy(w_ug[H:H + 1, :], p_b[H:H + 1, H:2 * H]).then_inc(s_fcopy, 1)

        def window_starts():
            eng.wait_ge(s_dst, 16)
            first = dst[0:1, :].rearrange("p (u t) -> p u t", t=TILES)[:, :, 0]
            eng.tensor_copy(win_start[:, :], first).then_inc(s_v, 1)
            eng.tensor_copy(startf[:, :], first).then_inc(s_sf, 1)

        def local_dst():
            eng.wait_ge(s_sp, 1)
            for k, c, bank in spans:
                def view(t):
                    return t[:, k * TILES:(k + c) * TILES].rearrange("p (u t) -> p u t", t=TILES)
                last = eng.tensor_tensor(view(dst_local), view(dst), bank[:, 0:c].unsqueeze(2).to_broadcast([P, c, TILES]),
                                         ALU.subtract)
            last.then_inc(s_v, 1)

        def largest():
            eng.wait_ge(s_v, 2)
            eng.tensor_reduce(spread[:, 0:1], dst_local[:, :], AX.X, ALU.max).then_inc(s_v, 1)

        def smallest():
            eng.tensor_reduce(spread[:, 1:2], dst_local[:, :], AX.X, ALU.min).then_inc(s_v, 1)

        extra = {0: window_starts, 1: local_dst}
        extra[min(6, GROUPS)] = largest
        extra[min(11, GROUPS + 1)] = smallest
        for g in range(GROUPS + 3):
            if g < GROUPS:
                s = g % SR
                eng.wait_ge(s_ab, g + 1)
                if g >= SR:
                    eng.wait_ge(s_stb[s], 16 * (g // SR))
                    eng.wait_ge(s_r1, g - SR + 1)
                eng.tensor_copy(ab[:, s, :, :].rearrange("p j n -> p (j n)"), p_ab[0:GP, g % 2, :]).then_inc(s_abc, 1)
            if 2 <= g < GROUPS + 2:
                k = g - 2
                eng.wait_ge(s_hi, k + 1)
                if k >= SR:
                    eng.wait_ge(s_mid, k - SR + 1)
                eng.tensor_tensor(rest[:, k % SR, :, :], ab[:, k % SR, :, 0:H], parts[:, k % SR, :, 0, :], ALU.subtract)\
                   .then_inc(s_r1, 1)
            if g >= 3:
                k = g - 3
                eng.wait_ge(s_mid, k + 1)
                eng.tensor_tensor(parts[:, k % SR, :, 2, :], rest[:, k % SR, :, :], parts[:, k % SR, :, 1, :],
                                  ALU.subtract).then_inc(s_lo, 1)
            if g in extra:
                extra[g]()
        eng.wait_ge(s_v, 4)
        eng.tensor_scalar(bad[:, 0:1], spread[:, 0:1], float(W), None, ALU.is_ge)
        eng.tensor_scalar(bad[:, 1:2], spread[:, 1:2], 0.0, None, ALU.is_lt).then_inc(s_v, 1)
        eng.wait_ge(s_v, 5)
        eng.tensor_tensor(bad[:, 2:3], bad[:, 0:1], bad[:, 1:2], ALU.add).then_inc(s_v, 1)
        eng.wait_ge(s_bad, 1)
        eng.tensor_copy(flag[:, :], p_b[0:1, 256:257]).then_inc(s_flag, 1)

    def wait_alone(eng, s, value):
        eng.wait_ge(s, value)
        eng.sem_inc(marks[str(eng.engine)], 1)

    def unit(turn, slot):
        return (turn + slot // RING, slot % RING)

    def col(u, width):
        return u[0] * (RING * width) + u[1] * width

    def turns(eng, body):
        with eng.Fori(0, TURNS - 1) as t:
            for slot in range(RING):
                body(unit(t, slot), unit(t, slot + 1))
        for slot in range(RING):
            body(unit(TURNS - 1, slot), unit(TURNS - 1, slot + 1) if slot + 1 < RING else None)

    def choose(eng, fast, general):
        eng.wait_ge(s_flag, 1)
        r = eng.value_load(flag[0:1, 0:1], min_val=0, max_val=2 * P)
        with eng.If(r == 0):
            fast(eng)
        with eng.Else():
            general(eng)

    def load_edges(eng, slot, first_edge, sem_above, sem_below):
        eng.dma_start(e_ring[0:H, slot, :], a["edgeT"][:, ds(first_edge, ECOLS)]).then_inc(sem_above, 16)
        eng.dma_start(e_ring[H:P, slot, 0:ELOW], a["edgeT"][:, ds(first_edge + ECOLS, ELOW)]).then_inc(sem_below, 16)

    def second_layer(eng, k, stop):
        n = PAIR_COLS[k]
        to = p_pre[:, k * P:k * P + n]
        return eng.matmul(to, hid[:, k * P:(k + 1) * P], w_ef[:, 0:n], start=True, stop=stop), to, n

    def window_sums(eng, slot):
        for k in range(TILES):
            last = eng.matmul(p_sum[:, 0:W], msg[:, k, :], hot_ring[:, slot, k, :], start=k == 0, stop=k == TILES - 1)
        return last

    def add_src(eng, slot):
        return eng.tensor_tensor(pre[:, :, :], p_pre[:, 0:TILES * H].rearrange("p (k n) -> p k n", n=H),
                                 b_ring[:, slot, :, :], ALU.add)

    def sync_fast(eng):
        def body(u, _):
            t, s = u
            eng.wait_ge(hid_mm[s], t + 1)
            load_edges(eng, s, col(u, UE), ea_in[s], eb_in[s])
            start = eng.value_load(win_start[0:1, ds(col(u, 1), 1)], min_val=0, max_val=N - 1)
            eng.wait_ge(pre_ok[s], t + 1)
            eng.dma_start(src_ring[:, s, :], a["src"][:, ds(col(u, TILES), TILES)]).then_inc(src_in[s], 16)
            for half in range(2):
                eng.dma_start(a_ring[half * H:(half + 1) * H, s, :, half * H:(half + 1) * H],
                              a_table[ds(start, W), :].rearrange("w (c n) -> w c n", c=3)).then_inc(a_in[s], 16)
        turns(eng, body)

    def pool_fast(eng):
        def body(u, _):
            t, s = u
            wait_alone(eng, src_in[s], 16 * t + 16)
            for k in range(TILES):
                eng.indirect_dma_start(b_ring[:, s, k, :], None, b_table,
                                       bass.IndirectOffsetOnAxis(ap=src_ring[:, s, k:k + 1], axis=0))\
                   .then_inc(b_in[s], 16)
        turns(eng, body)

    def hidden_mm(eng, u):
        t, s = u
        eng.wait_ge(ea_in[s], 16 * t + 16)
        eng.wait_ge(eb_in[s], 16 * t + 16)
        eng.matmul(p_hid[:, 0:ECOLS], w_e1[:, :], e_ring[:, s, :], start=True, stop=True).then_inc(hid_mm[s], 1)

    def hot_transpose(eng, u):
        t, s = u
        eng.wait_ge(hot_ok[s], t + 1)
        for k in range(PAIRS):
            last = eng.transpose(p_hot[:, k * P:(k + 1) * P],
                                 hot_ring[:, s, 2 * k:2 * k + 2, :].rearrange("p k w -> p (k w)"), ident[:, :])
        last.then_inc(hotT_mm[s], 1)

    def tensor_fast(eng):
        def body(u, nxt):
            t, s = u
            eng.wait_ge(hid_ok[s], t + 1)
            eng.wait_ge(hotT_ok[s], t + 1)
            eng.wait_ge(a_in[s], 32 * t + 32)
            for k in range(PAIRS):
                _, to, n = second_layer(eng, k, False)
                for c in range(3):
                    last = eng.matmul(to, hotT[:, k * P:(k + 1) * P], a_ring[:, s, c, 0:n], start=False, stop=c == 2)
            last.then_inc(pre_mm[s], 1)
            if nxt:
                hidden_mm(eng, nxt)
                hot_transpose(eng, nxt)
            eng.wait_ge(msg_ok[s], t + 1)
            eng.wait_ge(sum_ok[(s - 1) % RING], t + 1 if s == 0 else t + 2)
            window_sums(eng, s).then_inc(sum_mm[s], 1)
        hidden_mm(eng, (0, 0))
        hot_transpose(eng, (0, 0))
        turns(eng, body)

    def scalar_front(eng, u):
        t, s = u
        eng.wait_ge(hid_mm[s], t + 2)
        eng.activation(hid[:, :], p_hid[:, 0:ECOLS], ACT.Silu, bias=b_e1[:, :]).then_inc(hid_ok[s], 1)
        eng.wait_ge(hotT_mm[s], t + 1)
        eng.copy(hotT[:, :], p_hot[:, 0:ECOLS]).then_inc(hotT_ok[s], 1)

    def scalar_fast(eng):
        def body(u, nxt):
            t, s = u
            eng.wait_ge(pre_ok[s], t + 2)
            eng.activation(msg[:, :, 0:H], pre[:, :, :], ACT.Silu).then_inc(msg_ok[s], 1)
            if nxt:
                scalar_front(eng, nxt)
        scalar_front(eng, (0, 0))
        turns(eng, body)

    def one_hot(eng, u):
        t, s = u
        eng.tensor_tensor(hot_ring[:, s, 0:TILES, :],
                          dst_local[:, ds(col(u, TILES), TILES)].unsqueeze(2).to_broadcast([P, TILES, W]),
                          iota[:, :].unsqueeze(1).to_broadcast([P, TILES, W]), ALU.is_equal).then_inc(hot_ok[s], 1)

    def vector_fast(eng):
        def body(u, nxt):
            t, s = u
            if nxt:
                one_hot(eng, nxt)
            start = eng.value_load(win_start[0:1, ds(col(u, 1), 1)], min_val=0, max_val=N - 1)
            eng.wait_ge(pre_mm[s], t + 1)
            eng.wait_ge(b_in[s], 16 * TILES * t + 16 * TILES)
            add_src(eng, s).then_inc(pre_ok[s], 1)
            eng.wait_ge(sum_mm[s], t + 1)
            window = agg[:, ds(start, W)]
            wait_alone(eng, sum_ok[(s - 1) % RING], t + 1 if s == 0 else t + 2)
            eng.tensor_tensor(window, window, p_sum[:, 0:W], ALU.add).then_inc(sum_ok[s], 1)
        one_hot(eng, (0, 0))
        turns(eng, body)

    def sync_general(eng):
        with eng.Fori(0, UNITS) as u:
            wait_alone(eng, gen["done"], u + 1)
            load_edges(eng, 0, u * UE, gen["in"], gen["in"])
            eng.dma_start(src_ring[:, 0, :], a["src"][:, ds(u * TILES, TILES)]).then_inc(gen["in"], 16)
            eng.dma_start(dst_raw[:, :], a["dst"][:, ds(u * TILES, TILES)]).then_inc(gen["in"], 16)

    def pool_general(eng):
        with eng.Fori(0, UNITS) as u:
            wait_alone(eng, gen["in"], 64 * u + 64)
            for k in range(TILES):
                eng.indirect_dma_start(b_ring[:, 0, k, :], None, b_table,
                                       bass.IndirectOffsetOnAxis(ap=src_ring[:, 0, k:k + 1], axis=0))\
                   .then_inc(gen["b"], 16)
                eng.indirect_dma_start(a_rows[:, k, :, :].rearrange("p c n -> p (c n)"), None, a_table,
                                       bass.IndirectOffsetOnAxis(ap=dst_raw[:, k:k + 1], axis=0))\
                   .then_inc(gen["b"], 16)

    def tensor_general(eng):
        with eng.Fori(0, UNITS) as u:
            wait_alone(eng, gen["in"], 64 * u + 64)
            eng.matmul(p_hid[:, 0:ECOLS], w_e1[:, :], e_ring[:, 0, :], start=True, stop=True).then_inc(gen["hid_mm"], 1)
            wait_alone(eng, gen["hid"], u + 1)
            for k in range(PAIRS):
                last = second_layer(eng, k, True)[0]
            last.then_inc(gen["pre_mm"], 1)
            wait_alone(eng, gen["msg"], u + 1)
            with eng.Fori(0, WINDOWS) as k:
                wait_alone(eng, gen["hot"], u * WINDOWS + k + 1)
                window_sums(eng, 0).then_inc(gen["sum"], 1)

    def scalar_general(eng):
        with eng.Fori(0, UNITS) as u:
            wait_alone(eng, gen["hid_mm"], u + 1)
            eng.activation(hid[:, :], p_hid[:, 0:ECOLS], ACT.Silu, bias=b_e1[:, :]).then_inc(gen["hid"], 1)
            wait_alone(eng, gen["pre"], u + 1)
            eng.activation(msg[:, :, 0:H], pre[:, :, :], ACT.Silu).then_inc(gen["msg"], 1)

    def vector_general(eng):
        with eng.Fori(0, UNITS) as u:
            links = u * (5 + 2 * WINDOWS)
            wait_alone(eng, gen["b"], 32 * TILES * u + 32 * TILES)
            wait_alone(eng, gen["pre_mm"], u + 1)
            add_src(eng, 0).then_inc(gen["v"], 1)
            for c in range(3):
                wait_alone(eng, gen["v"], links + 1 + c)
                eng.tensor_tensor(pre[:, :, :], pre[:, :, :], a_rows[:, :, c, :], ALU.add)\
                   .then_inc(gen["v"] if c < 2 else gen["pre"], 1)
            eng.tensor_copy(dst_f[:, :], dst_raw[:, :]).then_inc(gen["v"], 1)
            eng.tensor_scalar(iota_k[:, :], iota[:, :], float(-W), None, ALU.add).then_inc(gen["v"], 1)
            wait_alone(eng, gen["v"], links + 5)
            with eng.Fori(0, WINDOWS) as k:
                here = links + 5 + 2 * k
                eng.tensor_scalar(iota_k[:, :], iota_k[:, :], float(W), None, ALU.add).then_inc(gen["v"], 1)
                wait_alone(eng, gen["v"], here + 1)
                eng.tensor_tensor(hot_ring[:, 0, 0:TILES, :], dst_f[:, :].unsqueeze(2).to_broadcast([P, TILES, W]),
                                  iota_k[:, :].unsqueeze(1).to_broadcast([P, TILES, W]), ALU.is_equal)\
                   .then_inc(gen["hot"], 1)
                wait_alone(eng, gen["sum"], u * WINDOWS + k + 1)
                window = agg[:, ds(k * W, W)]
                eng.tensor_tensor(window, window, p_sum[:, 0:W], ALU.add).then_inc(gen["v"], 1)
                wait_alone(eng, gen["v"], here + 2)
            eng.sem_inc(gen["done"], 1)

    with nc.Block() as block:
        @block.sync
        def _(eng):
            sync_nodes(eng)
            sync_tables_done(eng)
            choose(eng, sync_fast, sync_general)

        @block.gpsimd
        def _(eng):
            pool_nodes(eng)
            choose(eng, pool_fast, pool_general)

        @block.tensor
        def _(eng):
            tensor_nodes(eng)
            for s in range(RING):
                eng.sem_inc(hid_mm[s], 1)
            eng.wait_ge(s_w2, 16 * len(later_loads))
            eng.wait_ge(s_const, 4)
            eng.wait_ge(s_pool, 7)
            choose(eng, tensor_fast, tensor_general)

        @block.scalar
        def _(eng):
            scalar_nodes(eng)
            eng.wait_ge(s_w2, 16 * len(later_loads))
            choose(eng, scalar_fast, scalar_general)

        @block.vector
        def _(eng):
            vector_nodes(eng)
            for s in range(RING):
                eng.sem_inc(pre_ok[s], 1)
                eng.sem_inc(sum_ok[s], 1)
            eng.sem_inc(gen["done"], 1)
            eng.wait_ge(s_pool, 7)
            eng.wait_ge(s_const, 4)
            choose(eng, vector_fast, vector_general)


def update(nc, a, out, stack, v):
    sb, ps, sem = tools(nc, stack)
    GROUPS = v["GROUPS"]
    agg, w_ux, w_ug, b_u1, w_u2 = v["agg"], v["w_ux"], v["w_ug"], v["b_u1"], v["w_u2"]
    ln_g, ln_b = v["ln_g"], v["ln_b"]
    R = 6
    xT = sb("u_xT", [D, R, GN], F32)
    x = sb("u_x", [GP, R, GJ, D], F32)
    inv = sb("u_inv", [H, R, GN], F32)
    hid = sb("u_hid", [H + 1, R, GN], F32)
    y = sb("u_y", [GP, R, GJ, D], F32)
    z = sb("u_z", [GP, R, GJ, D], F32)
    o = sb("u_o", [GP, R, GJ, D], F32)
    stats = sb("u_stats", [GP, R, GJ, 6], F32)
    mv = sb("u_mv", [GP, R, 2, GJ, 2], F32)
    rstd = sb("u_rstd", [GP, R, 2, GJ], F32)
    shift = sb("u_shift", [GP, R, 2, GJ], F32)
    power = sb("u_power", [GP, GJ], F32)
    p_u = ps("p_u", [H, 2, BANK])
    p_d = ps("p_d", [P, 2, BANK])
    s_in = [sem(f"u_in{i}") for i in range(R)]
    s_out = [sem(f"u_out{i}") for i in range(R)]
    s_c = sem("u_constants")
    s_mean = sem("u_mean")
    s_some = sem("u_some")
    s_u = sem("u_psum")
    s_h = sem("u_hidden")
    s_d = sem("d_psum")
    s_mv = [sem("moments1"), sem("moments2")]
    s_rs = [sem("rstd1"), sem("rstd2")]
    s_z = sem("normed1")
    s_r2 = sem("residual2")
    s_o = sem("normed2")
    s_y = sem("y_sum")
    s_p = sem("pool_chain")
    s_v = sem("u_vector_chain")
    STEPS = range(GROUPS + 3)

    def rows(t, g):
        return t[g * GN:(g + 1) * GN, :].rearrange("(p j) n -> p j n", j=GJ)

    def wide(t):
        return t[0:GP, :].unsqueeze(1).to_broadcast([GP, GJ, D])

    def sync_part(eng):
        LAG = R + 2
        for n in range(GROUPS + LAG):
            g, r = n, n % R
            if g < GROUPS:
                if g >= R:
                    eng.wait_ge(s_u, g - R + 1)
                    eng.wait_ge(s_y, g - R + 1)
                    eng.wait_ge(s_r2, g - R + 1)
                eng.dma_start(xT[:, r, :], a["xT"][:, g * GN:(g + 1) * GN]).then_inc(s_in[r], 16)
                eng.dma_start(x[:, r, :, :], rows(a["x"], g)).then_inc(s_in[r], 16)
            if n >= LAG:
                k = n - LAG
                eng.wait_ge(s_o, k + 1)
                eng.dma_start(rows(out, k), o[:, k % R, :, :]).then_inc(s_out[k % R], 16)

    def pool_part(eng):
        chain = [0]

        def link(ins):
            chain[0] += 1
            ins.then_inc(s_p, 1)
            eng.wait_ge(s_p, chain[0])

        def scales(g, k):
            r = g % R
            eng.wait_ge(s_mv[k], g + 1)
            link(eng.tensor_scalar(rstd[:, r, k, :], mv[:, r, k, :, 1], EPS, None, ALU.add))
            link(eng.tensor_tensor(rstd[:, r, k, :], rstd[:, r, k, :], power[:, :], ALU.pow))
            link(eng.tensor_tensor(shift[:, r, k, :], mv[:, r, k, :, 0], rstd[:, r, k, :], ALU.mult))
            eng.tensor_scalar(shift[:, r, k, :], shift[:, r, k, :], -1.0, None, ALU.mult).then_inc(s_rs[k], 1)
            eng.wait_ge(s_rs[k], g + 1)

        def some(g):
            row = agg[H:H + 1, g * GN:(g + 1) * GN]
            eng.wait_ge(s_mean, g + 1)
            eng.tensor_scalar(row, row, 1.0, None, ALU.min).then_inc(s_some, 1)
            eng.wait_ge(s_some, g + 1)

        eng.memset(power[:, :], -0.5).then_inc(s_c, 1)
        eng.wait_ge(s_c, 3)
        some(0)
        for n in STEPS:
            if n + 1 < GROUPS:
                some(n + 1)
            if n < GROUPS:
                scales(n, 0)
            if 2 <= n < GROUPS + 2:
                scales(n - 2, 1)
            if 1 <= n < GROUPS + 1:
                g, r = n - 1, (n - 1) % R
                eng.wait_ge(s_z, g + 1)
                link(eng.tensor_tensor(z[:, r, :, :], z[:, r, :, :], wide(ln_g), ALU.mult))
                eng.tensor_tensor(z[:, r, :, :], z[:, r, :, :], x[:, r, :, :], ALU.add).then_inc(s_r2, 1)
                eng.wait_ge(s_r2, g + 1)

    def scalar_part(eng):
        def hidden(g):
            eng.wait_ge(s_u, g + 1)
            if g >= R:
                eng.wait_ge(s_d, g - R + 1)
            eng.activation(hid[0:H, g % R, :], p_u[:, g % 2, 0:GN], ACT.Silu, bias=b_u1[:, :]).then_inc(s_h, 1)

        def norm(g, k, to, done):
            r = g % R
            eng.wait_ge(s_rs[k], g + 1)
            if k == 1 and g >= R:
                eng.wait_ge(s_out[r], 16 * (g // R))
            for j in range(GJ):
                last = eng.activation(to[:, r, j, :], y[:, r, j, :], ACT.Identity,
                                      bias=shift[:, r, k, j:j + 1], scale=rstd[:, r, k, j:j + 1])
            last.then_inc(done, 1)

        eng.wait_ge(s_c, 3)
        hidden(0)
        for n in STEPS:
            if n + 1 < GROUPS:
                hidden(n + 1)
            if 1 <= n < GROUPS + 1:
                norm(n - 1, 0, z, s_z)
            if n >= 3:
                norm(n - 3, 1, o, s_o)
        for r in range(R):
            eng.wait_ge(s_out[r], 16 * len(range(r, GROUPS, R)))

    def tensor_part(eng):
        def up(g):
            r = g % R
            eng.wait_ge(s_in[r], 32 * (g // R + 1))
            eng.wait_ge(s_some, g + 1)
            if g >= 2:
                eng.wait_ge(s_h, g - 1)
            eng.matmul(p_u[:, g % 2, 0:GN], w_ux[:, :], xT[:, r, :], start=True, stop=False)
            eng.matmul(p_u[:, g % 2, 0:GN], w_ug[:, :], agg[0:H + 1, g * GN:(g + 1) * GN], start=False, stop=True)\
               .then_inc(s_u, 1)

        eng.wait_ge(s_c, 3)
        up(0)
        for g in range(GROUPS):
            if g + 1 < GROUPS:
                up(g + 1)
            eng.wait_ge(s_h, g + 1)
            if g >= 2:
                eng.wait_ge(s_y, g - 1)
            for j in range(GJ):
                last = eng.matmul(p_d[0:GP, g % 2, j * D:(j + 1) * D], hid[:, g % R, j:GN:GJ], w_u2[:, :],
                                  start=True, stop=True)
            last.then_inc(s_d, 1)

    def vector_part(eng):
        links = [0]

        def link(ins):
            links[0] += 1
            ins.then_inc(s_v, 1)
            eng.wait_ge(s_v, links[0])

        def mean(g):
            cols = slice(g * GN, (g + 1) * GN)
            r = g % R
            link(eng.tensor_scalar(inv[:, r, :], agg[H:2 * H, cols], 1.0, None, ALU.max))
            link(eng.reciprocal(inv[:, r, :], inv[:, r, :]))
            eng.tensor_tensor(agg[0:H, cols], agg[0:H, cols], inv[:, r, :], ALU.mult).then_inc(s_mean, 1)

        def moments(g, k):
            r = g % R
            for j in range(GJ):
                last = eng.bn_stats(stats[:, r, j, :], y[:, r, j, :])
            link(last)
            for j in range(GJ):
                last = eng.bn_aggr(mv[:, r, k, j, :], stats[:, r, j, :])
            last.then_inc(s_mv[k], 1)

        eng.memset(hid[H:H + 1, :, :], 1.0).then_inc(s_c, 2)
        mean(0)
        for n in STEPS:
            if n + 1 < GROUPS:
                mean(n + 1)
            if n < GROUPS:
                r = n % R
                eng.wait_ge(s_in[r], 32 * (n // R + 1))
                eng.wait_ge(s_d, n + 1)
                if n >= R:
                    eng.wait_ge(s_o, n - R + 1)
                eng.tensor_tensor(y[:, r, :, :], p_d[0:GP, n % 2, :].rearrange("p (j n) -> p j n", n=D),
                                  x[:, r, :, :], ALU.add).then_inc(s_y, 1)
                eng.wait_ge(s_y, n + 1)
                moments(n, 0)
            if 2 <= n < GROUPS + 2:
                g, r = n - 2, (n - 2) % R
                eng.wait_ge(s_r2, g + 1)
                link(eng.tensor_tensor(y[:, r, :, :], z[:, r, :, :], wide(ln_b), ALU.add))
                moments(g, 1)

    with nc.Block() as block:
        block.sync(sync_part)
        block.gpsimd(pool_part)
        block.scalar(scalar_part)
        block.tensor(tensor_part)
        block.vector(vector_part)


def _laid_out(inputs):
    g = {k.removeprefix("L0_gnn_"): np.asarray(t) for k, t in inputs.items()}
    keep = ["x", "node_W1", "node_b1", "node_b2", "edge_W1", "edge_b1", "edge_b2", "msg_W1", "msg_b1", "msg_b2",
            "upd_W1", "upd_b1", "upd_W2", "upd_b2", "ln_g", "ln_b"]
    d = {k: g[k] for k in keep}
    d["xT"] = g["x"].T
    d["edgeT"] = g["edge_attr_64"].T
    for k in ("node_W2", "edge_W2", "msg_W2"):
        d[k + "T"] = g[k].T
    for k in ("src", "dst"):
        d[k] = g[k].reshape(-1, TILES, P)[:, ORDER, :].reshape(-1, P).T
    return {k: np.ascontiguousarray(t) for k, t in d.items()}


def kernel(**inputs):
    import concourse.bacc as bacc
    from concourse.bass_utils import run_bass_kernel_spmd

    nc = bacc.Bacc("TRN2", target_bir_lowering=False, num_devices=1)
    arrays = {f"in_{k}": t for k, t in _laid_out(inputs).items()}
    aps = {k[3:]: nc.dram_tensor(k, t.shape, mybir.dt.from_np(t.dtype), kind="ExternalInput").ap()
           for k, t in arrays.items()}
    out = nc.dram_tensor("out", inputs["x"].shape, F32, kind="ExternalOutput").ap()
    build(nc, aps, out)
    r = run_bass_kernel_spmd(nc, [arrays], core_ids=[0])
    return r.results[0]["out"]
```

```python
import numpy as np
import concourse.bass as bass
import concourse.mybir as mybir
from contextlib import ExitStack

F32, BF16, I32 = mybir.dt.float32, mybir.dt.bfloat16, mybir.dt.int32
ALU, ACT, AX = mybir.AluOpType, mybir.ActivationFunctionType, mybir.AxisListType
ds = bass.ds

P = 128
H = 64
D = 128
W = 64
TILES = 5
UE = TILES * P
RING = 5
GN = 500
GJ = 4
GP = GN // GJ
GP16 = GP // 16 * 16
PAIRS = -(-TILES // 2)
PAIR_COLS = [2 * H] * (TILES // 2) + [H] * (TILES % 2)
ECOLS = PAIRS * P
ELOW = UE - ECOLS
ORDER = [k // 2 + (PAIRS if k % 2 else 0) for k in range(TILES)]
EPS = 1e-5
AT = dict(load=0, mean=0, up=1, hidden=2, down=3, sum=4, norm1=5, affine=6, sum2=7, norm2=8,
          store=13, stored=15)
LEAD = RING
BANK = 512


def build(nc, a, out):
    with ExitStack() as stack:
        program(nc, a, out, stack)


def program(nc, a, out, stack):
    def sb(name, shape, dt):
        return stack.enter_context(nc.sbuf_tensor(name, shape, dt))

    def ps(name, shape, dt=F32):
        return stack.enter_context(nc.psum_tensor(name, shape, dt))

    def sem(name):
        return stack.enter_context(nc.semaphore(name))

    N = a["x"].shape[0]
    E = a["edgeT"].shape[1]
    UNITS = E // UE
    TURNS = UNITS // RING
    GROUPS = N // GN
    WINDOWS = -(-N // W)
    NPAD = N + W
    assert UNITS * UE == E and TURNS * RING == UNITS and TURNS > 1 and GROUPS * GN == N
    UNITS_PG = UNITS * GN // N
    HEAD = UNITS_PG + LEAD
    ROUNDS = (UNITS - HEAD) // UNITS_PG
    REST = UNITS - HEAD - ROUNDS * UNITS_PG
    assert UNITS_PG * GROUPS == UNITS and not (HEAD % RING or UNITS_PG % RING)
    assert REST > max(AT.values()) and ROUNDS + 2 == GROUPS

    a_table = nc.dram_tensor("a_table", (NPAD, 3 * H), BF16, kind="Internal").ap()
    b_table = nc.dram_tensor("b_table", (N, H), F32, kind="Internal").ap()
    agg = sb("agg", [P, NPAD], F32)

    dst_local = sb("dst_local", [P, E // P], F32)
    win_start = sb("win_start", [1, UNITS], I32)
    flags = sb("flags", [1, 2], I32)
    iota = sb("iota", [P, W], F32)
    ident = sb("ident", [P, P], F32)
    w_e1 = sb("w_e1", [P, P], F32)
    w_ef = sb("w_ef", [P, P], F32)
    b_e1 = sb("b_e1", [P, 1], F32)
    w_n1 = sb("w_n1", [D, H], F32)
    n2T = sb("n2T", [H, H], F32)
    e2T = sb("e2T", [H, H], F32)
    m2T = sb("m2T", [H, H], F32)
    wm1 = sb("wm1", [H, 3, H], F32)
    u1g = sb("u1g", [H, H], F32)
    b_n1 = sb("b_n1", [H, 1], F32)
    vecs = sb("vecs", [H, 3], F32)
    b_m1 = sb("b_m1", [1, H], F32)
    ones = sb("ones", [P, P], F32)
    w_ux = sb("w_ux", [D, H], F32)
    w_ug = sb("w_ug", [H + 1, H], F32)
    b_u1 = sb("b_u1", [H, 1], F32)
    w_u2 = sb("w_u2", [H + 1, D], F32)
    ln_g = sb("ln_g", [P, D], F32)
    ln_b = sb("ln_b", [P, D], F32)
    w_ab = sb("w_ab", [P, 2 * H], F32)

    XR = 6
    SR = 6
    xT = sb("xT", [D, XR, GN], F32)
    n1 = sb("n1", [P, SR, GN], F32)
    ab = sb("ab", [GP, SR, 2, GJ, H], F32)
    rest = sb("rest", [GP, SR, GJ, H], F32)
    parts = sb("parts", [GP, SR, GJ, 3, H], BF16)
    pad = sb("pad", [W, 3 * H], BF16)
    dst = sb("dst", [P, E // P], I32)
    startf = sb("startf", [1, UNITS], F32)
    spread = sb("spread", [P, 2], F32)
    bad = sb("bad", [P, 3], F32)
    must = sb("must", [1, HEAD + (ROUNDS + 1) * UNITS_PG], F32)
    ahead = sb("ahead", [1, UNITS], F32)
    behind = sb("behind", [1, 2], F32)

    e_ring = sb("e_ring", [P, RING, ECOLS], F32)
    src_ring = sb("src_ring", [P, RING, TILES], I32)
    b_ring = sb("b_ring", [P, RING, TILES, H], F32)
    a_ring = sb("a_ring", [P, RING, 2, 3, H], BF16)
    hot_ring = sb("hot_ring", [P, RING, TILES + 1, W], F32)
    hotT = sb("hotT", [P, ECOLS], BF16)
    hid = sb("hid", [P, ECOLS], F32)
    pre = sb("pre", [P, TILES, H], F32)
    msg = sb("msg", [P, TILES, 2 * H], F32)
    dst_raw = sb("dst_raw", [P, TILES], I32)
    dst_f = sb("dst_f", [P, TILES], F32)
    a_rows = sb("a_rows", [P, TILES, 3, H], BF16)
    iota_k = sb("iota_k", [P, W], F32)

    u_xT = sb("u_xT", [D, GN], F32)
    u_x = sb("u_x", [GP, GJ, D], F32)
    inv = sb("inv", [H, GN], F32)
    mean = sb("mean", [H + 1, GN], F32)
    u_hid = sb("u_hid", [H + 1, GN], F32)
    y = sb("y", [GP, GJ, D], F32)
    z = sb("z", [GP, GJ, D], F32)
    o = sb("o", [GP, GJ, D], F32)
    stats = sb("stats", [GP, GJ, 6], F32)
    mv = sb("mv", [GP, GJ, 2], F32)
    rstd = sb("rstd", [GP, GJ], F32)
    var = sb("var", [GP, GJ], F32)
    half = sb("half", [GP, GJ], F32)
    bits = sb("bits", [GP, GJ], I32)

    p_hid = ps("p_hid", [P, BANK])
    p_hot = ps("p_hot", [P, BANK])
    p_pre = ps("p_pre", [P, BANK])
    p_sum = ps("p_sum", [P, BANK])
    p_h = ps("p_h", [H, 2, BANK])
    p_ab = ps("p_ab", [P, 2, BANK])
    p_w, p_b = p_hid, p_hot
    p_up, p_down = p_h[:, 0, 0:GN], p_ab[0:GP, 0, :]
    spans = [(k, min(BANK, UNITS - k), bank) for k, bank in zip(range(0, UNITS, BANK), (p_pre, p_sum))]
    assert spans[-1][0] + spans[-1][1] == UNITS
    CUT = BANK // 4
    pieces = [(k + at, min(CUT, c - at), at, bank) for k, c, bank in spans for at in range(0, c, CUT)]
    ends = sb("ends", [P, 2, len(pieces)], F32)

    s_wx = sem("x_layer_in")
    s_w = sem("weights_in")
    s_bias = sem("biases_in")
    s_dst = sem("dst_in")
    s_x = [sem(f"x_in{i}") for i in range(XR)]
    s_const = sem("constants")
    s_pool = sem("pool_constants")
    s_fold = sem("folded")
    s_fcopy = sem("folded_copied")
    s_h = sem("hidden_psum")
    s_n1 = sem("hidden_done")
    s_ab = sem("ab_psum")
    s_abc = sem("ab_copied")
    s_hi = sem("hi_done")
    s_r1 = sem("rest_done")
    s_mid = sem("mid_done")
    s_lo = sem("lo_done")
    s_sta = [sem(f"a_stored{i}") for i in range(SR)]
    s_stb = [sem(f"b_stored{i}") for i in range(SR)]
    s_pad = sem("pad_stored")
    s_sf = sem("start_float")
    s_table = sem("a_table_done")
    s_ends = sem("piece_ends")
    s_local = sem("local_dst")
    s_sp = sem("start_spread")
    s_v = sem("vector_chain")
    s_bad = sem("bad_sum")
    s_flag = sem("flag_done")

    def ring_sems(name):
        return [sem(f"{name}{i}") for i in range(RING)]

    ea_in, eb_in, src_in, a_in, b_in = (ring_sems(n) for n in ("ea_in", "eb_in", "src_in", "a_in", "b_in"))
    hid_mm = ring_sems("hid_mm")
    hid_ok = ring_sems("hid_ok")
    hot_ok = ring_sems("hot_ok")
    hotT_mm = ring_sems("hotT_mm")
    hotT_ok = ring_sems("hotT_ok")
    pre_mm = ring_sems("pre_mm")
    pre_ok = ring_sems("pre_ok")
    msg_ok = ring_sems("msg_ok")
    sum_mm = ring_sems("sum_mm")
    sum_ok = ring_sems("sum_ok")
    marks = {str(e.engine): sem(f"mark{n}") for n, e in enumerate((nc.sync, nc.gpsimd, nc.tensor, nc.scalar, nc.vector))}
    gen = {n: sem("gen_" + n) for n in ("in", "b", "hid_mm", "hid", "pre_mm", "pre", "msg", "hot", "sum", "done", "v")}

    x_layer = [(w_n1[:, :], a["node_W1"]), (b_n1[:, :], a["node_b1"].unsqueeze(1))]
    fold_loads = [(wm1[:, :, :], a["msg_W1"].rearrange("(w k) n -> k w n", k=H)), (n2T[:, :], a["node_W2T"]),
                  (e2T[:, :], a["edge_W2T"]), (m2T[:, :], a["msg_W2T"]), (u1g[:, :], a["upd_W1"][D:D + H, :])]
    bias_loads = [(vecs[:, 0:1], a["node_b2"].unsqueeze(1)), (vecs[:, 1:2], a["edge_b2"].unsqueeze(1)),
                  (vecs[:, 2:3], a["msg_b2"].unsqueeze(1)), (b_m1[:, :], a["msg_b1"].unsqueeze(0))]
    later_loads = [
        (w_e1[0:H, 0:H], a["edge_W1"]), (w_e1[H:P, H:P], a["edge_W1"]),
        (b_e1[0:H, :], a["edge_b1"].unsqueeze(1)), (b_e1[H:P, :], a["edge_b1"].unsqueeze(1)),
        (w_ux[:, :], a["upd_W1"][0:D, :]), (b_u1[:, :], a["upd_b1"].unsqueeze(1)),
        (w_u2[0:H, :], a["upd_W2"]), (w_u2[H:H + 1, :], a["upd_b2"].unsqueeze(0)),
        (ln_g[:, :], a["ln_g"].partition_broadcast(P)), (ln_b[:, :], a["ln_b"].partition_broadcast(P)),
    ]
    s_w2 = sem("later_weights_in")
    s_ux = sem("up_x_in")
    s_um = sem("up_mean")
    s_uu = sem("up_hidden_psum")
    s_uh = sem("up_hidden")
    s_ud = sem("up_psum")
    s_uv = sem("up_vector_chain")
    s_uo = sem("up_result")
    s_out = sem("out_stored")

    def sync_nodes(eng):
        LAG = XR + SR
        for to, of in x_layer:
            eng.dma_start(to, of).then_inc(s_wx, 16)
        for g in range(GROUPS + LAG):
            if g < GROUPS:
                if g >= XR:
                    eng.wait_ge(s_h, g - XR + 1)
                eng.dma_start(xT[:, g % XR, :], a["xT"][:, g * GN:(g + 1) * GN]).then_inc(s_x[g % XR], 16)
            if g == 1:
                eng.dma_start(dst[:, :], a["dst"]).then_inc(s_dst, 16)
            if g >= LAG:
                k = g - LAG
                eng.wait_ge(s_lo, k + 1)
                rows = a_table[k * GN:(k + 1) * GN, :].rearrange("(p j) n -> p (j n)", j=GJ)
                for part in (slice(0, GP16), slice(GP16, GP)):
                    eng.dma_start(rows[part, :], parts[part, k % SR, :, :, :].rearrange("p j c n -> p (j c n)"))\
                       .then_inc(s_sta[k % SR], 16)

    def scalar_tables_done(eng):
        for i in range(SR):
            eng.wait_ge(s_sta[i], 32 * len(range(i, GROUPS, SR)))
        eng.wait_ge(s_pad, 16)
        eng.sem_inc(s_table, 1)

    def pool_nodes(eng):
        for to, of in bias_loads:
            eng.dma_start(to, of).then_inc(s_bias, 16)
        eng.iota(iota[:, :], [[1, W]], base=0, channel_multiplier=0,
                 allow_small_or_imprecise_dtypes=True).then_inc(s_pool, 1)
        eng.memset(ident[:, :], 0.0).then_inc(s_pool, 1)
        eng.memset(pad[:, :], 0.0).then_inc(s_pool, 1)
        eng.memset(a_ring[:, :, :, :, :], 0.0).then_inc(s_pool, 1)
        eng.wait_ge(s_pool, 4)
        eng.memset(e_ring[H:P, :, ELOW:ECOLS], 0.0).then_inc(s_pool, 1)
        eng.wait_ge(s_pool, 5)
        eng.memset(hot_ring[:, :, TILES, :], 0.0).then_inc(s_pool, 1)
        eng.iota(must[:, HEAD:], [[GN, ROUNDS + 1], [0, UNITS_PG]], base=GN, channel_multiplier=0,
                 allow_small_or_imprecise_dtypes=True).then_inc(s_pool, 1)
        eng.wait_ge(s_pool, 7)
        eng.affine_select(out=ident[:, :], in_=ident[:, :], compare_op=ALU.not_equal, fill=1.0,
                          base=0, pattern=[[-1, P]], channel_multiplier=1).then_inc(s_pool, 1)
        eng.dma_start(a_table[N:NPAD, :], pad[:, :]).then_inc(s_pad, 16)
        eng.memset(agg[:, :], 0.0).then_inc(s_pool, 1)
        for g in range(GROUPS):
            eng.wait_ge(s_abc, g + 1)
            eng.dma_start(b_table[g * GN:(g + 1) * GN, :].rearrange("(p j) n -> p j n", j=GJ),
                          ab[:, g % SR, 1, :, :]).then_inc(s_stb[g % SR], 16)
        for i in range(SR):
            eng.wait_ge(s_stb[i], 16 * len(range(i, GROUPS, SR)))

    def scalar_nodes(eng):
        for to, of in fold_loads:
            eng.dma_start(to, of).then_inc(s_w, 16)
        eng.wait_ge(s_wx, 16 * len(x_layer))
        for g in range(max(GROUPS + 3, len(later_loads))):
            if g < GROUPS:
                eng.wait_ge(s_h, g + 1)
                if g >= SR:
                    eng.wait_ge(s_ab, g - SR + 1)
                eng.activation(n1[0:H, g % SR, :], p_h[:, g % 2, 0:GN], ACT.Silu, bias=b_n1[:, :]).then_inc(s_n1, 1)
            if 2 <= g < GROUPS + 2:
                k = g - 2
                eng.wait_ge(s_abc, k + 1)
                if k >= SR:
                    eng.wait_ge(s_sta[k % SR], 32 * (k // SR))
                eng.copy(parts[:, k % SR, :, 0, :], ab[:, k % SR, 0, :, :]).then_inc(s_hi, 1)
            if 3 <= g < GROUPS + 3:
                k = g - 3
                eng.wait_ge(s_r1, k + 1)
                eng.copy(parts[:, k % SR, :, 1, :], rest[:, k % SR, :, :]).then_inc(s_mid, 1)
            if g < len(later_loads):
                to, of = later_loads[g]
                eng.dma_start(to, of).then_inc(s_w2, 16)

    def tensor_nodes(eng):
        eng.wait_ge(s_wx, 16 * len(x_layer))
        mm = eng.matmul

        def node_hidden(g):
            eng.wait_ge(s_x[g % XR], 16 * (g // XR + 1))
            if g >= 2:
                eng.wait_ge(s_n1, g - 1)
            mm(p_h[:, g % 2, 0:GN], w_n1[:, :], xT[:, g % XR, :], start=True, stop=True).then_inc(s_h, 1)

        node_hidden(0)
        eng.wait_ge(s_w, 16 * len(fold_loads))
        eng.wait_ge(s_bias, 16 * len(bias_loads))
        eng.wait_ge(s_const, 2)
        mm(p_w[0:H, 0:2 * H], n2T[:, :], wm1[:, 0:2, :], start=True, stop=True)
        mm(p_w[0:H, 2 * H:3 * H], e2T[:, :], wm1[:, 2, :], start=True, stop=True)
        mm(p_w[0:H, 3 * H:4 * H], m2T[:, :], u1g[:, :], start=True, stop=True)
        row = p_b[H:H + 1, 0:H]
        mm(row, vecs[:, 0:1], wm1[:, 0, :], start=True, stop=False)
        mm(row, vecs[:, 0:1], wm1[:, 1, :], start=False, stop=False)
        mm(row, vecs[:, 1:2], wm1[:, 2, :], start=False, stop=False)
        mm(row, ones[0:1, 0:1], b_m1[:, :], start=False, stop=True)
        mm(p_b[H:H + 1, H:2 * H], vecs[:, 2:3], u1g[:, :], start=True, stop=True).then_inc(s_fold, 1)
        for g in range(GROUPS):
            if g + 1 < GROUPS:
                node_hidden(g + 1)
            eng.wait_ge(s_n1, g + 1)
            if g == 0:
                eng.wait_ge(s_fcopy, 7)
            if g >= 2:
                eng.wait_ge(s_abc, g - 1)
            for j in range(GJ):
                last = mm(p_ab[0:GP, g % 2, j * 2 * H:(j + 1) * 2 * H], n1[:, g % SR, j:GN:GJ], w_ab[:, :],
                          start=True, stop=True)
            last.then_inc(s_ab, 1)
            if g == 1:
                eng.wait_ge(s_sf, 1)
                for k, c, bank in spans:
                    last = mm(bank[:, 0:c], ones[0:1, :], startf[:, k:k + c], start=True, stop=True)
                last.then_inc(s_sp, 1)
            if g == min(22, GROUPS - 1):
                eng.wait_ge(s_v, 8)
                mm(p_b[0:1, 256:257], bad[:, 2:3], ones[:, 0:1], start=True, stop=True).then_inc(s_bad, 1)

    def vector_nodes(eng):
        eng.memset(ones[:, :], 1.0).then_inc(s_const, 1)
        eng.memset(n1[H:P, :, :], 1.0).then_inc(s_const, 1)
        for t in (w_ef, w_e1):
            eng.memset(t[0:H, H:P], 0.0)
            eng.memset(t[H:P, 0:H], 0.0)
        eng.memset(w_ab[H:P, :], 0.0).then_inc(s_fcopy, 1)
        eng.memset(must[:, 0:HEAD], 0.0)
        eng.memset(u_hid[H:H + 1, :], 1.0)
        eng.memset(msg[:, :, H:2 * H], 1.0).then_inc(s_const, 1)
        eng.wait_ge(s_fcopy, 1)
        eng.wait_ge(s_fold, 1)
        eng.tensor_copy(w_ab[0:H, :], p_w[0:H, 0:2 * H]).then_inc(s_fcopy, 1)
        eng.tensor_copy(w_ab[H:H + 1, 0:H], p_b[H:H + 1, 0:H]).then_inc(s_fcopy, 1)
        eng.tensor_copy(w_ef[0:H, 0:H], p_w[0:H, 2 * H:3 * H]).then_inc(s_fcopy, 1)
        eng.tensor_copy(w_ef[H:P, H:P], p_w[0:H, 2 * H:3 * H]).then_inc(s_fcopy, 1)
        eng.tensor_copy(w_ug[0:H, :], p_w[0:H, 3 * H:4 * H]).then_inc(s_fcopy, 1)
        eng.tensor_copy(w_ug[H:H + 1, :], p_b[H:H + 1, H:2 * H]).then_inc(s_fcopy, 1)

        def window_starts():
            eng.wait_ge(s_dst, 16)
            first = dst[0:1, :].rearrange("p (u t) -> p u t", t=TILES)[:, :, 0]
            eng.tensor_copy(win_start[:, :], first).then_inc(s_v, 1)
            eng.tensor_copy(startf[:, :], first).then_inc(s_sf, 1)

        def local_dst(piece):
            k, c, at, bank = pieces[piece]

            def step():
                def view(t):
                    return t[:, k * TILES:(k + c) * TILES].rearrange("p (u t) -> p u t", t=TILES)
                eng.wait_ge(s_sp, 1)
                eng.tensor_tensor(view(dst_local), view(dst), bank[:, at:at + c].unsqueeze(2).to_broadcast([P, c, TILES]),
                                  ALU.subtract).then_inc(s_local, 1)
            return step

        def schedule():
            eng.wait_ge(s_pool, 8)
            eng.wait_ge(s_v, 3)
            eng.tensor_tensor(ahead[:, :], startf[:, :], must[:, 0:UNITS], ALU.subtract).then_inc(s_v, 1)
            eng.wait_ge(s_v, 4)
            eng.tensor_reduce(behind[:, 0:1], ahead[:, :], AX.X, ALU.min).then_inc(s_v, 1)
            eng.wait_ge(s_v, 5)
            eng.tensor_scalar(behind[:, 1:2], behind[:, 0:1], 0.0, None, ALU.is_lt).then_inc(s_v, 1)

        def marks_of_bad():
            eng.wait_ge(s_v, 6)
            eng.tensor_scalar(bad[:, 0:1], spread[:, 0:1], float(W), None, ALU.is_ge)
            eng.tensor_scalar(bad[:, 1:2], spread[:, 1:2], 0.0, None, ALU.is_lt).then_inc(s_v, 1)
            eng.wait_ge(s_v, 7)
            eng.tensor_tensor(bad[:, 2:3], bad[:, 0:1], bad[:, 1:2], ALU.add).then_inc(s_v, 1)

        def piece_end(which, op, piece):
            k, c, _, _ = pieces[piece]

            def step():
                eng.wait_ge(s_local, piece + 1)
                eng.tensor_reduce(ends[:, which, piece:piece + 1], dst_local[:, k * TILES:(k + c) * TILES], AX.X, op)\
                   .then_inc(s_ends, 1)
            return step

        def both_ends():
            eng.wait_ge(s_ends, 2 * len(pieces))
            eng.tensor_reduce(spread[:, 0:1], ends[:, 0, :], AX.X, ALU.max).then_inc(s_v, 1)
            eng.tensor_reduce(spread[:, 1:2], ends[:, 1, :], AX.X, ALU.min).then_inc(s_v, 1)

        beside = [(0, window_starts)]
        steps = [local_dst(n) for n in range(len(pieces))]
        steps += [piece_end(0, ALU.max, n) for n in range(len(pieces))]
        steps += [piece_end(1, ALU.min, n) for n in range(len(pieces))]
        steps += [both_ends, schedule, marks_of_bad]
        beside += [(min(3 + n, GROUPS - 1), step) for n, step in enumerate(steps)]
        for g in range(GROUPS + 4):
            if 3 <= g < GROUPS + 3:
                k = g - 3
                eng.wait_ge(s_hi, k + 1)
                if k >= SR:
                    eng.wait_ge(s_mid, k - SR + 1)
                eng.tensor_tensor(rest[:, k % SR, :, :], ab[:, k % SR, 0, :, :], parts[:, k % SR, :, 0, :], ALU.subtract)\
                   .then_inc(s_r1, 1)
            if g >= 4:
                k = g - 4
                eng.wait_ge(s_mid, k + 1)
                eng.tensor_tensor(parts[:, k % SR, :, 2, :], rest[:, k % SR, :, :], parts[:, k % SR, :, 1, :],
                                  ALU.subtract).then_inc(s_lo, 1)
            if g < GROUPS:
                s = g % SR
                eng.wait_ge(s_ab, g + 1)
                if g >= SR:
                    eng.wait_ge(s_stb[s], 16 * (g // SR))
                    eng.wait_ge(s_r1, g - SR + 1)
                eng.tensor_copy(ab[:, s, :, :, :], p_ab[0:GP, g % 2, :].rearrange("p (j t n) -> p t j n", t=2, n=H))\
                   .then_inc(s_abc, 1)
            for at, step in beside:
                if at == g:
                    step()
        eng.wait_ge(s_bad, 1)
        eng.tensor_copy(flags[:, 0:1], p_b[0:1, 256:257])
        eng.tensor_tensor(flags[:, 1:2], p_b[0:1, 256:257], behind[:, 1:2], ALU.add).then_inc(s_flag, 1)

    def wait_alone(eng, s, value):
        eng.wait_ge(s, value)
        eng.sem_inc(marks[str(eng.engine)], 1)

    def unit(turn, slot):
        return (turn + slot // RING, slot % RING)

    def col(u, width):
        return u[0] * (RING * width) + u[1] * width

    def turns(eng, body):
        with eng.Fori(0, TURNS - 1) as t:
            for slot in range(RING):
                body(eng, unit(t, slot), unit(t, slot + 1))
        for slot in range(RING):
            body(eng, unit(TURNS - 1, slot), unit(TURNS - 1, slot + 1) if slot + 1 < RING else None)

    def turns_with_updates(eng, body, steps):
        def stretch(g, units, last):
            for i in range(units):
                first = HEAD // RING + g * (UNITS_PG // RING)
                u, nxt = (unit(first + k // RING, k % RING) for k in (i, i + 1))
                body(eng, u, None if last and i == units - 1 else nxt)
                if i in steps:
                    steps[i](eng, g, u)

        with eng.Fori(0, HEAD // RING) as t:
            for slot in range(RING):
                body(eng, unit(t, slot), unit(t, slot + 1))
        with eng.Fori(0, ROUNDS) as g:
            stretch(g, UNITS_PG, False)
        stretch(ROUNDS, REST, True)
        for i in sorted(steps):
            steps[i](eng, GROUPS - 1, (TURNS - 1, RING - 1))

    def choose(eng, body, before, general, steps):
        eng.wait_ge(s_flag, 1)
        outside = eng.value_load(flags[0:1, 0:1], min_val=0, max_val=2 * P)
        off_schedule = eng.value_load(flags[0:1, 1:2], min_val=0, max_val=2 * P + 1)
        with eng.If(off_schedule == 0):
            before(eng)
            turns_with_updates(eng, body, steps)
        with eng.Else():
            with eng.If(outside == 0):
                before(eng)
                turns(eng, body)
            with eng.Else():
                general(eng)
            with eng.Fori(0, GROUPS) as g:
                for i in sorted(steps):
                    steps[i](eng, g, None)

    def load_edges(eng, slot, first_edge, sem_above, sem_below):
        eng.dma_start(e_ring[0:H, slot, :], a["edgeT"][:, ds(first_edge, ECOLS)]).then_inc(sem_above, 16)
        eng.dma_start(e_ring[H:P, slot, 0:ELOW], a["edgeT"][:, ds(first_edge + ECOLS, ELOW)]).then_inc(sem_below, 16)

    def second_layer(eng, k, stop):
        n = PAIR_COLS[k]
        to = p_pre[:, k * P:k * P + n]
        return eng.matmul(to, hid[:, k * P:(k + 1) * P], w_ef[:, 0:n], start=True, stop=stop), to, n

    def window_sums(eng, slot):
        for k in range(TILES):
            last = eng.matmul(p_sum[:, 0:W], msg[:, k, :], hot_ring[:, slot, k, :], start=k == 0, stop=k == TILES - 1)
        return last

    def add_src(eng, slot):
        return eng.tensor_tensor(pre[:, :, :], p_pre[:, 0:TILES * H].rearrange("p (k n) -> p k n", n=H),
                                 b_ring[:, slot, :, :], ALU.add)

    def sync_unit(eng, u, _):
        t, s = u
        start = eng.value_load(win_start[0:1, ds(col(u, 1), 1)], min_val=0, max_val=N - 1)
        eng.wait_ge(pre_ok[s], t + 1)
        eng.dma_start(src_ring[:, s, :], a["src"][:, ds(col(u, TILES), TILES)]).then_inc(src_in[s], 16)
        eng.wait_ge(hid_mm[s], t + 1)
        load_edges(eng, s, col(u, UE), ea_in[s], eb_in[s])
        eng.wait_ge(s_table, 1)
        for half in range(2):
            eng.dma_start(a_ring[half * H:(half + 1) * H, s, half, :, :].rearrange("p c n -> p (c n)"),
                          a_table[ds(start, W), :]).then_inc(a_in[s], 16)

    def pool_unit(eng, u, _):
        t, s = u
        wait_alone(eng, src_in[s], 16 * t + 16)
        for k in range(TILES):
            eng.indirect_dma_start(b_ring[:, s, k, :], None, b_table,
                                   bass.IndirectOffsetOnAxis(ap=src_ring[:, s, k:k + 1], axis=0))\
               .then_inc(b_in[s], 16)

    def hidden_mm(eng, u):
        t, s = u
        eng.wait_ge(ea_in[s], 16 * t + 16)
        eng.wait_ge(eb_in[s], 16 * t + 16)
        eng.matmul(p_hid[:, 0:ECOLS], w_e1[:, :], e_ring[:, s, :], start=True, stop=True).then_inc(hid_mm[s], 1)

    def hot_transpose(eng, u):
        t, s = u
        eng.wait_ge(hot_ok[s], t + 1)
        for k in range(PAIRS):
            last = eng.transpose(p_hot[:, k * P:(k + 1) * P],
                                 hot_ring[:, s, 2 * k:2 * k + 2, :].rearrange("p k w -> p (k w)"), ident[:, :])
        last.then_inc(hotT_mm[s], 1)

    def tensor_unit(eng, u, nxt):
        t, s = u
        eng.wait_ge(hid_ok[s], t + 1)
        eng.wait_ge(hotT_ok[s], t + 1)
        eng.wait_ge(a_in[s], 32 * t + 32)
        for k in range(PAIRS):
            _, to, n = second_layer(eng, k, False)
            for c in range(3):
                last = eng.matmul(to, hotT[:, k * P:(k + 1) * P], a_ring[:, s, 0:n // H, c, :], start=False, stop=c == 2)
        last.then_inc(pre_mm[s], 1)
        if nxt:
            hidden_mm(eng, nxt)
            hot_transpose(eng, nxt)
        eng.wait_ge(msg_ok[s], t + 1)
        eng.wait_ge(sum_ok[(s - 1) % RING], t + 1 if s == 0 else t + 2)
        window_sums(eng, s).then_inc(sum_mm[s], 1)

    def tensor_first(eng):
        hidden_mm(eng, (0, 0))
        hot_transpose(eng, (0, 0))

    def scalar_front(eng, u):
        t, s = u
        eng.wait_ge(hid_mm[s], t + 2)
        eng.activation(hid[:, :], p_hid[:, 0:ECOLS], ACT.Silu, bias=b_e1[:, :]).then_inc(hid_ok[s], 1)
        eng.wait_ge(hotT_mm[s], t + 1)
        eng.copy(hotT[:, :], p_hot[:, 0:ECOLS]).then_inc(hotT_ok[s], 1)

    def scalar_unit(eng, u, nxt):
        t, s = u
        eng.wait_ge(pre_ok[s], t + 2)
        eng.activation(msg[:, :, 0:H], pre[:, :, :], ACT.Silu).then_inc(msg_ok[s], 1)
        if nxt:
            scalar_front(eng, nxt)

    def scalar_first(eng):
        scalar_front(eng, (0, 0))

    def one_hot(eng, u):
        t, s = u
        eng.tensor_tensor(hot_ring[:, s, 0:TILES, :],
                          dst_local[:, ds(col(u, TILES), TILES)].unsqueeze(2).to_broadcast([P, TILES, W]),
                          iota[:, :].unsqueeze(1).to_broadcast([P, TILES, W]), ALU.is_equal).then_inc(hot_ok[s], 1)

    def vector_unit(eng, u, nxt):
        t, s = u
        if nxt:
            one_hot(eng, nxt)
        start = eng.value_load(win_start[0:1, ds(col(u, 1), 1)], min_val=0, max_val=N - 1)
        eng.wait_ge(pre_mm[s], t + 1)
        eng.wait_ge(b_in[s], 16 * TILES * t + 16 * TILES)
        add_src(eng, s).then_inc(pre_ok[s], 1)
        eng.wait_ge(sum_mm[s], t + 1)
        window = agg[:, ds(start, W)]
        wait_alone(eng, sum_ok[(s - 1) % RING], t + 1 if s == 0 else t + 2)
        eng.tensor_tensor(window, window, p_sum[:, 0:W], ALU.add).then_inc(sum_ok[s], 1)

    def vector_first(eng):
        one_hot(eng, (0, 0))

    def nothing(eng):
        pass

    def up_load(eng, g, u):
        eng.dma_start(u_xT[:, :], a["xT"][:, ds(g * GN, GN)]).then_inc(s_ux, 16)
        eng.dma_start(u_x[:, :, :], a["x"][ds(g * GN, GN), :].rearrange("(p j) n -> p j n", j=GJ)).then_inc(s_ux, 16)

    def up_store(eng, g, u):
        wait_alone(eng, s_uo, g + 1)
        eng.dma_start(out[ds(g * GN, GN), :].rearrange("(p j) n -> p j n", j=GJ), o[:, :, :]).then_inc(s_out, 16)

    def up_stored(eng, g, u):
        wait_alone(eng, s_out, g * 16 + 16)

    def up_layer1(eng, g, u):
        wait_alone(eng, s_ux, g * 32 + 32)
        eng.matmul(p_up, w_ux[:, :], u_xT[:, :], start=True, stop=False)
        wait_alone(eng, s_um, g + 1)
        eng.matmul(p_up, w_ug[:, :], mean[:, :], start=False, stop=True).then_inc(s_uu, 1)

    def up_layer2(eng, g, u):
        wait_alone(eng, s_uh, g + 1)
        for j in range(GJ):
            last = eng.matmul(p_down[:, j * D:(j + 1) * D], u_hid[:, j:GN:GJ], w_u2[:, :], start=True, stop=True)
        last.then_inc(s_ud, 1)

    def up_hidden(eng, g, u):
        wait_alone(eng, s_uu, g + 1)
        eng.activation(u_hid[0:H, :], p_up, ACT.Silu, bias=b_u1[:, :]).then_inc(s_uh, 1)

    NEWTON = 3
    ROOT_GUESS = 0x5F3759DF
    MOMENTS = 5 + 3 * NEWTON
    LINKS = 7 + 2 * MOMENTS

    def link(eng, g, k, ins):
        ins.then_inc(s_uv, 1)
        wait_alone(eng, s_uv, g * LINKS + k)

    def up_mean(eng, g, u):
        cols = ds(g * GN, GN)
        if u:
            wait_alone(eng, sum_ok[u[1]], u[0] + 2)
        link(eng, g, 1, eng.tensor_scalar(inv[:, :], agg[H:2 * H, cols], 1.0, None, ALU.max))
        link(eng, g, 2, eng.reciprocal(inv[:, :], inv[:, :]))
        eng.tensor_scalar(mean[H:H + 1, :], agg[H:H + 1, cols], 1.0, None, ALU.min)
        eng.tensor_tensor(mean[0:H, :], agg[0:H, cols], inv[:, :], ALU.mult).then_inc(s_um, 1)

    def moments(eng, g, k):
        for j in range(GJ):
            last = eng.bn_stats(stats[:, j, :], y[:, j, :])
        link(eng, g, k, last)
        for j in range(GJ):
            last = eng.bn_aggr(mv[:, j, :], stats[:, j, :])
        link(eng, g, k + 1, last)
        link(eng, g, k + 2, eng.tensor_scalar(var[:, :], mv[:, :, 1], EPS, None, ALU.add))
        link(eng, g, k + 3, eng.tensor_scalar(bits[:, :], var[:, :].bitcast(I32), 1, None, ALU.logical_shift_right))
        link(eng, g, k + 4, eng.tensor_scalar(rstd[:, :].bitcast(I32), bits[:, :], -1, ROOT_GUESS, ALU.mult, ALU.add))
        for n in range(NEWTON):
            m = k + 5 + 3 * n
            link(eng, g, m, eng.tensor_tensor(half[:, :], rstd[:, :], rstd[:, :], ALU.mult))
            link(eng, g, m + 1, eng.scalar_tensor_tensor(half[:, :], half[:, :], -0.5, var[:, :], ALU.mult, ALU.mult))
            link(eng, g, m + 2, eng.scalar_tensor_tensor(rstd[:, :], half[:, :], 1.5, rstd[:, :], ALU.add, ALU.mult))

    def normed(eng, to):
        for j in range(GJ):
            last = eng.tensor_scalar(to[:, j, :], y[:, j, :], mv[:, j, 0:1], rstd[:, j:j + 1], ALU.subtract, ALU.mult)
        return last

    def wide(t):
        return t[0:GP, :].unsqueeze(1).to_broadcast([GP, GJ, D])

    def up_sum(eng, g, u):
        wait_alone(eng, s_ud, g + 1)
        link(eng, g, 3, eng.tensor_tensor(y[:, :, :], p_down.rearrange("p (j n) -> p j n", n=D), u_x[:, :, :], ALU.add))
        moments(eng, g, 4)

    def up_norm1(eng, g, u):
        link(eng, g, 4 + MOMENTS, normed(eng, z))

    def up_affine(eng, g, u):
        link(eng, g, 5 + MOMENTS, eng.tensor_tensor(z[:, :, :], z[:, :, :], wide(ln_g), ALU.mult))
        link(eng, g, 6 + MOMENTS, eng.tensor_tensor(z[:, :, :], z[:, :, :], wide(ln_b), ALU.add))

    def up_sum2(eng, g, u):
        link(eng, g, 7 + MOMENTS, eng.tensor_tensor(y[:, :, :], z[:, :, :], u_x[:, :, :], ALU.add))
        moments(eng, g, 8 + MOMENTS)

    def up_norm2(eng, g, u):
        normed(eng, o).then_inc(s_uo, 1)

    pool_updates = {}
    sync_updates = {AT["load"]: up_load, AT["store"]: up_store, AT["stored"]: up_stored}
    tensor_updates = {AT["up"]: up_layer1, AT["down"]: up_layer2}
    scalar_updates = {AT["hidden"]: up_hidden}
    vector_updates = {AT["mean"]: up_mean, AT["sum"]: up_sum, AT["norm1"]: up_norm1, AT["affine"]: up_affine,
                      AT["sum2"]: up_sum2, AT["norm2"]: up_norm2}

    def sync_general(eng):
        eng.wait_ge(s_table, 1)
        with eng.Fori(0, UNITS) as u:
            wait_alone(eng, gen["done"], u + 1)
            load_edges(eng, 0, u * UE, gen["in"], gen["in"])
            eng.dma_start(src_ring[:, 0, :], a["src"][:, ds(u * TILES, TILES)]).then_inc(gen["in"], 16)
            eng.dma_start(dst_raw[:, :], a["dst"][:, ds(u * TILES, TILES)]).then_inc(gen["in"], 16)

    def pool_general(eng):
        with eng.Fori(0, UNITS) as u:
            wait_alone(eng, gen["in"], 64 * u + 64)
            for k in range(TILES):
                eng.indirect_dma_start(b_ring[:, 0, k, :], None, b_table,
                                       bass.IndirectOffsetOnAxis(ap=src_ring[:, 0, k:k + 1], axis=0))\
                   .then_inc(gen["b"], 16)
                eng.indirect_dma_start(a_rows[:, k, :, :].rearrange("p c n -> p (c n)"), None, a_table,
                                       bass.IndirectOffsetOnAxis(ap=dst_raw[:, k:k + 1], axis=0))\
                   .then_inc(gen["b"], 16)

    def tensor_general(eng):
        with eng.Fori(0, UNITS) as u:
            wait_alone(eng, gen["in"], 64 * u + 64)
            eng.matmul(p_hid[:, 0:ECOLS], w_e1[:, :], e_ring[:, 0, :], start=True, stop=True).then_inc(gen["hid_mm"], 1)
            wait_alone(eng, gen["hid"], u + 1)
            for k in range(PAIRS):
                last = second_layer(eng, k, True)[0]
            last.then_inc(gen["pre_mm"], 1)
            wait_alone(eng, gen["msg"], u + 1)
            with eng.Fori(0, WINDOWS) as k:
                wait_alone(eng, gen["hot"], u * WINDOWS + k + 1)
                window_sums(eng, 0).then_inc(gen["sum"], 1)

    def scalar_general(eng):
        with eng.Fori(0, UNITS) as u:
            wait_alone(eng, gen["hid_mm"], u + 1)
            eng.activation(hid[:, :], p_hid[:, 0:ECOLS], ACT.Silu, bias=b_e1[:, :]).then_inc(gen["hid"], 1)
            wait_alone(eng, gen["pre"], u + 1)
            eng.activation(msg[:, :, 0:H], pre[:, :, :], ACT.Silu).then_inc(gen["msg"], 1)

    def vector_general(eng):
        with eng.Fori(0, UNITS) as u:
            links = u * (5 + 2 * WINDOWS)
            wait_alone(eng, gen["b"], 32 * TILES * u + 32 * TILES)
            wait_alone(eng, gen["pre_mm"], u + 1)
            add_src(eng, 0).then_inc(gen["v"], 1)
            for c in range(3):
                wait_alone(eng, gen["v"], links + 1 + c)
                eng.tensor_tensor(pre[:, :, :], pre[:, :, :], a_rows[:, :, c, :], ALU.add)\
                   .then_inc(gen["v"] if c < 2 else gen["pre"], 1)
            eng.tensor_copy(dst_f[:, :], dst_raw[:, :]).then_inc(gen["v"], 1)
            eng.tensor_scalar(iota_k[:, :], iota[:, :], float(-W), None, ALU.add).then_inc(gen["v"], 1)
            wait_alone(eng, gen["v"], links + 5)
            with eng.Fori(0, WINDOWS) as k:
                here = links + 5 + 2 * k
                eng.tensor_scalar(iota_k[:, :], iota_k[:, :], float(W), None, ALU.add).then_inc(gen["v"], 1)
                wait_alone(eng, gen["v"], here + 1)
                eng.tensor_tensor(hot_ring[:, 0, 0:TILES, :], dst_f[:, :].unsqueeze(2).to_broadcast([P, TILES, W]),
                                  iota_k[:, :].unsqueeze(1).to_broadcast([P, TILES, W]), ALU.is_equal)\
                   .then_inc(gen["hot"], 1)
                wait_alone(eng, gen["sum"], u * WINDOWS + k + 1)
                window = agg[:, ds(k * W, W)]
                eng.tensor_tensor(window, window, p_sum[:, 0:W], ALU.add).then_inc(gen["v"], 1)
                wait_alone(eng, gen["v"], here + 2)
            eng.sem_inc(gen["done"], 1)

    with nc.Block() as block:
        @block.sync
        def _(eng):
            sync_nodes(eng)
            choose(eng, sync_unit, nothing, sync_general, sync_updates)
            eng.wait_ge(s_out, 16 * GROUPS)

        @block.gpsimd
        def _(eng):
            pool_nodes(eng)
            choose(eng, pool_unit, nothing, pool_general, pool_updates)

        @block.tensor
        def _(eng):
            tensor_nodes(eng)
            for s in range(RING):
                eng.sem_inc(hid_mm[s], 1)
            eng.wait_ge(s_w2, 16 * len(later_loads))
            eng.wait_ge(s_const, 3)
            eng.wait_ge(s_pool, 9)
            choose(eng, tensor_unit, tensor_first, tensor_general, tensor_updates)

        @block.scalar
        def _(eng):
            scalar_nodes(eng)
            scalar_tables_done(eng)
            eng.wait_ge(s_w2, 16 * len(later_loads))
            choose(eng, scalar_unit, scalar_first, scalar_general, scalar_updates)

        @block.vector
        def _(eng):
            vector_nodes(eng)
            for s in range(RING):
                eng.sem_inc(pre_ok[s], 1)
                eng.sem_inc(sum_ok[s], 1)
            eng.sem_inc(gen["done"], 1)
            eng.wait_ge(s_pool, 9)
            choose(eng, vector_unit, vector_first, vector_general, vector_updates)


def _laid_out(inputs):
    g = {k.removeprefix("L0_gnn_"): np.asarray(t) for k, t in inputs.items()}
    keep = ["x", "node_W1", "node_b1", "node_b2", "edge_W1", "edge_b1", "edge_b2", "msg_W1", "msg_b1", "msg_b2",
            "upd_W1", "upd_b1", "upd_W2", "upd_b2", "ln_g", "ln_b"]
    d = {k: g[k] for k in keep}
    d["xT"] = g["x"].T
    d["edgeT"] = g["edge_attr_64"].T
    for k in ("node_W2", "edge_W2", "msg_W2"):
        d[k + "T"] = g[k].T
    for k in ("src", "dst"):
        d[k] = g[k].reshape(-1, TILES, P)[:, ORDER, :].reshape(-1, P).T
    return {k: np.ascontiguousarray(t) for k, t in d.items()}


def kernel(**inputs):
    import concourse.bacc as bacc
    from concourse.bass_utils import run_bass_kernel_spmd

    nc = bacc.Bacc("TRN2", target_bir_lowering=False, num_devices=1)
    arrays = {f"in_{k}": t for k, t in _laid_out(inputs).items()}
    aps = {k[3:]: nc.dram_tensor(k, t.shape, mybir.dt.from_np(t.dtype), kind="ExternalInput").ap()
           for k, t in arrays.items()}
    out = nc.dram_tensor("out", inputs["x"].shape, F32, kind="ExternalOutput").ap()
    build(nc, aps, out)
    r = run_bass_kernel_spmd(nc, [arrays], core_ids=[0])
    return r.results[0]["out"]
```
